# Optimizing a Trainium2 kernel written in Bass

```python
import numpy as np
import jax
import jax.numpy as jnp

def _softmax(x, axis=-1):
    return jax.nn.softmax(x, axis=axis)

def _gelu(x):
    return jax.nn.gelu(x, approximate=True)

def _silu(x):
    return jax.nn.silu(x)

def _sigmoid(x):
    return jax.nn.sigmoid(x)

def _layernorm(x, axis=-1, eps=1e-05):
    m = jnp.mean(x, axis=axis, keepdims=True)
    v = jnp.var(x, axis=axis, keepdims=True)
    return (x - m) / jnp.sqrt(v + eps)

def _scatter_add(tgt, idx, src, axis=0):
    return tgt.at[idx].add(src)

def _segment_sum(src, seg, n):
    return jax.ops.segment_sum(src, seg, n)
kernel_name = 'mk_xattn_ffn_d1_seqx_r8_5c8827'

def setup_inputs(seed: int=0):
    np.random.seed(seed)
    _w = jnp.asarray

    def _rec_inputs():
        import jax
        import jax.numpy as jnp
        _rk = jax.random.key(seed)
        x = -0.0003929 + 0.9999 * jax.random.normal(jax.random.fold_in(_rk, 1), (1, 1024, 128), jnp.float32)
        _lenS = 1024 - jax.random.randint(jax.random.fold_in(_rk, 7), (1,), 0, max(1, 1024 // 4) + 1, jnp.int32)
        _lenS2 = 6404 - jax.random.randint(jax.random.fold_in(_rk, 8), (1,), 0, max(1, 6404 // 4) + 1, jnp.int32)
        _ctx_1024P = jax.random.normal(jax.random.fold_in(_rk, 11), (1, 16, 128), jnp.float32)
        _ctx_1024c = jax.random.dirichlet(jax.random.fold_in(_rk, 511), 0.3 * jnp.ones((16,), jnp.float32), (1, 6404))
        _ctx_1024t = jnp.einsum('bsk,bkd->bsd', _ctx_1024c, _ctx_1024P)
        _ctx_1024t = _ctx_1024t * jax.lax.rsqrt(jnp.mean(jnp.square(_ctx_1024t)) + 1e-12) * 0.953939
        ctx_1024 = -1.39393e-06 + 0.999914 * (_ctx_1024t + 0.3 * jax.random.normal(jax.random.fold_in(_rk, 611), (1, 6404, 128), jnp.float32))
        return (x, ctx_1024)
    x, ctx_1024 = _rec_inputs()

    def _L0_xattn_setup():
        import jax, jax.numpy as jnp
        import numpy as np
        B, C_LEN, Q_LEN, D = (8, 256, 64, 128)
        key = jax.random.key(seed)
        ks = jax.random.split(key, 10)
        scale = 1.0 / np.sqrt(D)
        return {'c': jax.random.normal(ks[0], (B, C_LEN, D), dtype=jnp.float32), 'q': jax.random.normal(ks[1], (B, Q_LEN, D), dtype=jnp.float32), 'w_cq': jax.random.normal(ks[2], (D,), dtype=jnp.float32) * scale, 'b_cq': jax.random.normal(ks[3], (), dtype=jnp.float32) * scale, 'w_c': jax.random.normal(ks[4], (D,), dtype=jnp.float32) * scale, 'b_c': jax.random.normal(ks[5], (), dtype=jnp.float32) * scale, 'w_q': jax.random.normal(ks[6], (D,), dtype=jnp.float32) * scale, 'b_q': jax.random.normal(ks[7], (), dtype=jnp.float32) * scale, 'W_l': jax.random.normal(ks[8], (D, 4 * D), dtype=jnp.float32) * (1.0 / np.sqrt(4 * D)), 'b_l': jax.random.normal(ks[9], (D,), dtype=jnp.float32) * (1.0 / np.sqrt(4 * D))}
    _L0_xattn_all = _L0_xattn_setup()
    _L0_xattn_in = {k: v for k, v in _L0_xattn_all.items() if k in ('w_cq', 'b_cq', 'w_c', 'b_c', 'w_q', 'b_q', 'W_l', 'b_l')}
    del _L0_xattn_all

    def _L0_ffn_setup():
        import jax, jax.numpy as jnp
        import numpy as np
        B, S, H, F, E = (4, 256, 128, 512, 8)
        key = jax.random.key(seed)
        ks = jax.random.split(key, 8)
        s = 1.0 / np.sqrt(H)
        sf = 1.0 / np.sqrt(F)
        return {'x': jax.random.normal(ks[0], (B, S, H), jnp.float32), 'wr': jax.random.uniform(ks[1], (H, E), jnp.float32, -s, s), 'br': jax.random.uniform(ks[2], (E,), jnp.float32, -s, s), 'w1': jax.random.uniform(ks[3], (E, H, F), jnp.float32, -s, s), 'b1': jax.random.uniform(ks[4], (E, F), jnp.float32, -s, s), 'w2': jax.random.uniform(ks[5], (E, F, H), jnp.float32, -sf, sf), 'b2': jax.random.uniform(ks[6], (E, H), jnp.float32, -sf, sf)}
    _L0_ffn_all = _L0_ffn_setup()
    _L0_ffn_in = {k: v for k, v in _L0_ffn_all.items() if k in ('wr', 'br', 'w1', 'b1', 'w2', 'b2')}
    del _L0_ffn_all
    return {'x': x, 'ctx_1024': ctx_1024, 'L0_xattn_w_cq': _L0_xattn_in['w_cq'], 'L0_xattn_b_cq': _L0_xattn_in['b_cq'], 'L0_xattn_w_c': _L0_xattn_in['w_c'], 'L0_xattn_b_c': _L0_xattn_in['b_c'], 'L0_xattn_w_q': _L0_xattn_in['w_q'], 'L0_xattn_b_q': _L0_xattn_in['b_q'], 'L0_xattn_W_l': _L0_xattn_in['W_l'], 'L0_xattn_b_l': _L0_xattn_in['b_l'], 'L0_ffn_wr': _L0_ffn_in['wr'], 'L0_ffn_br': _L0_ffn_in['br'], 'L0_ffn_w1': _L0_ffn_in['w1'], 'L0_ffn_b1': _L0_ffn_in['b1'], 'L0_ffn_w2': _L0_ffn_in['w2'], 'L0_ffn_b2': _L0_ffn_in['b2']}

def reference(x, ctx_1024, L0_xattn_w_cq, L0_xattn_b_cq, L0_xattn_w_c, L0_xattn_b_c, L0_xattn_w_q, L0_xattn_b_q, L0_xattn_W_l, L0_xattn_b_l, L0_ffn_wr, L0_ffn_br, L0_ffn_w1, L0_ffn_b1, L0_ffn_w2, L0_ffn_b2):
    import jax
    import jax.numpy as jnp

    def _L0_xattn_ref(c, q, w_cq, b_cq, w_c, b_c, w_q, b_q, W_l, b_l):
        import jax, jax.numpy as jnp
        import numpy as np
        B, C_LEN, Q_LEN, D = (8, 256, 64, 128)
        cq = jnp.einsum('bcd,bqd,d->bcq', c, q, w_cq) + b_cq
        s = (c @ w_c + b_c)[:, :, None] + (q @ w_q + b_q)[:, None, :] + cq
        a = jax.nn.softmax(s, axis=2)
        c2q_att = jnp.einsum('bcq,bqd->bcd', a, q)
        b_att = jax.nn.softmax(jnp.max(s, axis=2), axis=1)
        q2c_att = jnp.einsum('bc,bcd->bd', b_att, c)[:, None, :]
        x = jnp.concatenate([c, c2q_att, c * c2q_att, c * q2c_att], axis=-1)
        z = x @ W_l.T + b_l
        return z

    def _L0_ffn_ref(x, wr, br, w1, b1, w2, b2):
        import jax, jax.numpy as jnp
        import numpy as np
        B, S, H, F, E = (4, 256, 128, 512, 8)
        scores = jnp.einsum('bsh,he->bse', x, wr) + br
        expert_id = jnp.argmax(scores, axis=-1)
        h = jnp.einsum('bsh,ehf->ebsf', x, w1) + b1[:, None, None, :]
        h = jax.nn.gelu(h, approximate=False)
        y = jnp.einsum('ebsf,efh->ebsh', h, w2) + b2[:, None, None, :]
        one_hot = jax.nn.one_hot(expert_id, E, dtype=x.dtype)
        out = jnp.einsum('ebsh,bse->bsh', y, one_hot)
        return out
    x = x + _L0_xattn_ref(_layernorm(x, axis=-1), ctx_1024, L0_xattn_w_cq, L0_xattn_b_cq, L0_xattn_w_c, L0_xattn_b_c, L0_xattn_w_q, L0_xattn_b_q, L0_xattn_W_l, L0_xattn_b_l)
    x = x + _L0_ffn_ref(_layernorm(x, axis=-1), L0_ffn_wr, L0_ffn_br, L0_ffn_w1, L0_ffn_b1, L0_ffn_w2, L0_ffn_b2)
    return x

_drawn_inputs = setup_inputs


def setup_inputs(seed=0):
    import zlib

    import numpy as np

    out = dict(_drawn_inputs(seed))
    spreads = {}
    factors = {'L0_ffn_b1': 3.742}
    for name, (base, spread) in spreads.items():
        noise = np.random.default_rng([zlib.crc32(name.encode()), seed]).standard_normal(out[name].shape)
        drawn = base * np.exp(spread * noise) if base else spread * noise
        out[name] = jnp.asarray(drawn.astype(out[name].dtype))
    for name, factor in factors.items():
        out[name] = (out[name] * factor).astype(out[name].dtype)
    return out
```

```python
import concourse.bass as bass
from concourse import mybir
from contextlib import ExitStack
import math

F32 = mybir.dt.float32
F16 = mybir.dt.float16
ACT = mybir.ActivationFunctionType
ALU = mybir.AluOpType
AX = mybir.AxisListType

P = 128


def build(nc, x, ctxT, ctx, w_cq, w_c, w_q, b3, wlT, b_l, wr, br, w1, b1, w2, b2, out):
    N, D = x.shape
    Q = ctx.shape[0]
    E, _, F = w1.shape
    T = N // P
    QT = -(-Q // P)
    QF = Q // P
    QTAIL = Q - QF * P
    QP = QT * P
    FC = F // P
    CH = 512
    NCH = -(-Q // CH)
    GR = 2 * CH
    NG = -(-Q // GR)
    TG = 4
    NT = -(-QT // TG)
    GS = 16.0
    LIFT = 14 * math.log(2.0)
    EPS = 1e-5

    def cols(k, size):
        return k * size, min((k + 1) * size, Q)

    def tiles(k):
        return range(k * TG, min((k + 1) * TG, QT))

    es = ExitStack()
    with es:
        def sb(name, shape, dt=F32):
            return es.enter_context(nc.sbuf_tensor(name, shape, dt))

        def sem(name):
            return es.enter_context(nc.semaphore(name))

        x_sb = sb("x_sb", [P, T, D])
        c_sb = sb("c_sb", [P, T, D])
        cT = sb("cT", [P, N])
        g32 = sb("g32", [P, N])
        gh = sb("gh", [P, N], F16)
        gl = sb("gl", [P, N], F16)
        stageT = sb("stageT", [P, Q])
        stageN = sb("stageN", [P, QT * D])
        qTh = sb("qTh", [P, Q], F16)
        qTl = sb("qTl", [P, Q], F16)
        qn = sb("qn", [P, QT, 2, D], F16)
        S = sb("S", [P, Q])
        Pm = sb("Pm", [P, QP])
        PTs = sb("PTs", [P, 3, 2, CH], F16)
        a_sb = sb("a_sb", [P, N])
        idf = sb("idf", [P, P])
        ones = sb("ones", [P, P])
        mv = sb("mv", [P, T, 2])
        st = sb("st", [P, T, 6])
        rstd = sb("rstd", [P, T])
        sc1 = sb("sc1", [P, T])
        sc2 = sb("sc2", [P, T])
        mxp = sb("mxp", [P, NG])
        mx = sb("mx", [P, T])
        negb = sb("negb", [P, T])
        Lp = sb("Lp", [P, T * NG])
        Ls = sb("Ls", [P, 1])
        Li = sb("Li", [P, 1])
        otmp = sb("otmp", [P, D])
        vecs = sb("vecs", [P, 4])
        vecs16 = sb("vecs16", [P, 2])
        b3s = sb("b3s", [3, 1])
        b3r = sb("b3r", [3, T])
        wl = sb("wl", [P, 4, D])
        blr = sb("blr", [1, D])
        Mrow = sb("Mrow", [P, T])
        m1 = sb("m1", [P, 1])
        m2 = sb("m2", [1, 1])
        nM = sb("nM", [P, 1])
        eb = sb("eb", [P, T])
        es1 = sb("es1", [P, 1])
        Bi = sb("Bi", [P, 1])
        q2c = sb("q2c", [P, 1])
        wc2 = sb("wc2", [P, D])
        wrs = sb("wrs", [P, E])
        brs = sb("brs", [1, E])
        rsc = sb("rsc", [P, T, E])
        rmx = sb("rmx", [P, T])
        iota_e = sb("iota_e", [P, E])
        cand = sb("cand", [P, T, E])
        oneh = sb("oneh", [P, T, E])
        b1s = sb("b1s", [P, E, FC])
        b2s = sb("b2s", [1, E, D])
        aT, caT = S[:, 0:N], S[:, N:2 * N]
        hT = S[:, 2 * N:2 * N + 2 * FC * CH].rearrange("p (a f n) -> p a f n", a=2, f=FC)
        x1 = Pm[:, 0:N].rearrange("p (t d) -> p t d", d=D)
        x2n = Pm[:, N:2 * N].rearrange("p (t d) -> p t d", d=D)
        x2T = Pm[:, 2 * N:3 * N]

        psS = [es.enter_context(nc.psum_tensor(f"psS{i}", [P, GR], F32)) for i in range(2)]
        psT = [es.enter_context(nc.psum_tensor(f"psT{i}", [P, CH], F32)) for i in range(3)]
        psO = es.enter_context(nc.psum_tensor("psO", [P, CH], F32))
        bankS = [psS[0][:, 0:CH], psS[0][:, CH:GR], psS[1][:, 0:CH], psS[1][:, CH:GR]]

        x_landed = sem("x_landed")
        small_landed = sem("small_landed")
        qT_landed = [sem(f"qT_landed{n}") for n in range(NG)]
        qn_landed = [sem(f"qn_landed{n}") for n in range(NG)]
        qtail_landed = sem("qtail_landed")
        late_landed = sem("late_landed")
        w1_landed = sem("w1_landed")
        w2_landed = sem("w2_landed")
        out_landed = sem("out_landed")
        consts_ready = sem("consts_ready")
        tail_zeroed = sem("tail_zeroed")
        var_ready = sem("var_ready")
        sqrt_ready = sem("sqrt_ready")
        c_ready = sem("c_ready")
        cT_in_psum = sem("cT_in_psum")
        g_ready = sem("g_ready")
        qTh_ready = sem("qTh_ready")
        qTl_ready = sem("qTl_ready")
        qnh_ready = sem("qnh_ready")
        qn_ready = sem("qn_ready")
        scores_in_psum = sem("scores_in_psum")
        scores_out = sem("scores_out")
        max_parts = sem("max_parts")
        negb_ready = sem("negb_ready")
        exp_done = sem("exp_done")
        pT_in_psum = sem("pT_in_psum")
        high_done = sem("high_done")
        low_done = sem("low_done")
        pv_done = sem("pv_done")
        o_small = sem("o_small")
        o_out = sem("o_out")
        post_pe = sem("post_pe")
        post_dve = sem("post_dve")
        post_act = sem("post_act")
        dve_chain = sem("dve_chain")
        h_in_psum = sem("h_in_psum")
        gelu_done = sem("gelu_done")
        y_in_psum = sem("y_in_psum")
        y_added = sem("y_added")

        block = es.enter_context(nc.Block())

        NP = T // 2

        @block.sync
        def _(sp):
            sp.dma_start(x_sb[:, :, :], x.rearrange("(t p) d -> p t d", p=P)).then_inc(x_landed, 16)
            for n in range(NG):
                a, b = cols(n, GR)
                sp.dma_start(stageT[:, a:b], ctxT[:, a:b]).then_inc(qT_landed[n], 16)
            for n in range(NG):
                j0, j1 = n * 8, min(n * 8 + 8, QF)
                sp.dma_start(stageN[:, j0 * D:j1 * D].rearrange("p (j d) -> p j d", d=D),
                             ctx[j0 * P:j1 * P, :].rearrange("(j p) d -> p j d", p=P)).then_inc(qn_landed[n], 16)
            sp.wait_ge(tail_zeroed, 1)
            sp.dma_start(stageN[0:QTAIL, QF * D:QT * D], ctx[QF * P:Q, :]).then_inc(qtail_landed, 16)
            sp.dma_start(wl[:, :, :], wlT.rearrange("(k p) o -> p k o", p=P)).then_inc(late_landed, 16)
            sp.wait_ge(qTl_ready, NG)
            sp.dma_start(stageT[:, 0:E * F].rearrange("p (e f) -> p e f", f=F),
                         w1.rearrange("e h f -> h e f")).then_inc(w1_landed, 16)
            sp.wait_ge(qn_ready, NG)
            sp.dma_start(stageN[:, 0:E * FC * D].rearrange("p (e k d) -> p e k d", k=FC, d=D),
                         w2.rearrange("e (k p) d -> p e k d", p=P)).then_inc(w2_landed, 16)
            sp.wait_ge(y_added, 2 * E * 4 + 1)
            sp.dma_start(out.rearrange("(t p) d -> p t d", p=P), x1[:, :, :]).then_inc(out_landed, 16)
            sp.wait_ge(out_landed, 16)

        NSMALL = 6
        NLATE = 4

        @block.gpsimd
        def _(pool):
            nc.gpsimd.memset(idf[:, :], 0.0).then_inc(consts_ready, 1)
            nc.gpsimd.memset(ones[:, :], 1.0).then_inc(consts_ready, 1)
            pool.wait_ge(consts_ready, 2)
            nc.gpsimd.affine_select(out=idf[:, :], in_=idf[:, :], compare_op=ALU.not_equal, fill=1.0, base=0,
                                    pattern=[[-1, P]], channel_multiplier=1).then_inc(consts_ready, 1)
            nc.gpsimd.memset(stageN[:, QF * D:QT * D], 0.0).then_inc(tail_zeroed, 1)
            nc.gpsimd.memset(Pm[:, Q:QP], 0.0).then_inc(consts_ready, 1)
            for e in range(E):
                nc.gpsimd.memset(iota_e[:, e:e + 1], float(e)).then_inc(consts_ready, 1)
            for n in range(NG):
                j0, j1 = n * 8, min(n * 8 + 8, QT)
                pool.wait_ge(qn_landed[n], 16)
                if n == NG - 1:
                    pool.wait_ge(qtail_landed, 16)
                src = stageN[:, j0 * D:j1 * D].rearrange("p (j d) -> p j d", d=D)
                nc.gpsimd.tensor_copy(qn[:, j0:j1, 0, :], src).then_inc(qnh_ready, 1)
                pool.wait_ge(qnh_ready, n + 1)
                nc.gpsimd.tensor_tensor(qn[:, j0:j1, 1, :], src, qn[:, j0:j1, 0, :],
                                        ALU.subtract).then_inc(qn_ready, 1)

        @block.scalar
        def _(act):
            for i, v in enumerate((w_cq, w_q, w_c)):
                act.dma_start(vecs[:, i:i + 1], v.rearrange("(p o) -> p o", o=1)).then_inc(small_landed, 16)
            act.dma_start(b3s[:, :], b3.rearrange("(p o) -> p o", o=1)).then_inc(small_landed, 16)
            act.dma_start(blr[:, :], b_l.rearrange("(o d) -> o d", o=1)).then_inc(small_landed, 16)
            act.dma_start(brs[:, :], br.rearrange("(o d) -> o d", o=1)).then_inc(small_landed, 16)
            act.dma_start(wrs[:, :], wr).then_inc(late_landed, 16)
            act.dma_start(b2s[:, :, :], b2.rearrange("(o e) d -> o e d", o=1)).then_inc(late_landed, 16)
            act.dma_start(b1s[:, :, :], b1.rearrange("p (e k) -> p e k", k=FC)).then_inc(late_landed, 16)
            act.wait_ge(var_ready, 1)
            nc.scalar.activation(sc1[:, :], sc2[:, :], ACT.Sqrt).then_inc(sqrt_ready, 1)
            for n in range(NG):
                a, b = cols(n, GR)
                act.wait_ge(qT_landed[n], 16)
                nc.scalar.copy(qTh[:, a:b], stageT[:, a:b]).then_inc(qTh_ready, 1)

            def exp_piece(t, e, has_prev):
                a, b = cols(e, GR)
                if e == 0:
                    act.wait_ge(negb_ready, t + 1)
                if has_prev:
                    act.wait_ge(pT_in_psum, (t - 1) * NT + min(2 * e + 2, NT))
                nc.scalar.activation(Pm[:, a:b], S[:, a:b], ACT.Exp, bias=negb[:, bass.ds(t, 1)],
                                     accum_out=Lp[:, bass.ds(t * NG + e, 1)]).then_inc(exp_done, 1)

            def high(t, k, has_prev):
                w = len(tiles(k)) * P
                act.wait_ge(pT_in_psum, t * NT + k + 1)
                if k >= 3:
                    act.wait_ge(pv_done, t * NT + k - 2)
                elif has_prev and k == 0:
                    act.wait_ge(pv_done, t * NT)
                nc.scalar.copy(PTs[:, k % 3, 0, 0:w], psT[k % 3][:, 0:w]).then_inc(high_done, 1)

            def step(t, has_prev, has_next):
                for k in range(NT):
                    if k % 2 == 0 and k // 2 + 2 < NG:
                        exp_piece(t, k // 2 + 2, has_prev)
                    high(t, k, has_prev)
                    if has_next and k in (NT - 3, NT - 2):
                        exp_piece(t + 1, k - (NT - 3), True)

            exp_piece(0, 0, False)
            exp_piece(0, 1, False)
            step(0, False, True)
            with act.Fori(1, T - 1) as t:
                step(t, True, True)
            step(T - 1, True, False)
            act.wait_ge(post_dve, 3)
            nc.scalar.activation(eb[:, :], Mrow[:, :], ACT.Exp, bias=nM[:, :],
                                 accum_out=es1[:, :]).then_inc(post_act, 1)
            act.wait_ge(post_dve, 7)
            nc.scalar.activation(sc1[:, :], sc2[:, :], ACT.Sqrt).then_inc(post_act, 1)
            act.wait_ge(late_landed, 16 * NLATE)
            for i in range(2 * E):
                e, h = i // 2, i % 2
                for f in range(FC):
                    act.wait_ge(h_in_psum, i * FC + f + 1)
                    if i >= 2 and f == 0:
                        act.wait_ge(y_in_psum, (i - 1) * 4)
                    nc.scalar.activation(hT[:, i % 2, f, :], bankS[f], ACT.Gelu,
                                         bias=b1s[:, e, f:f + 1]).then_inc(gelu_done, 1)

        @block.vector
        def _(dve):
            chain = [0]

            def link(ins):
                chain[0] += 1
                ins.then_inc(dve_chain, 1)
                dve.wait_ge(dve_chain, chain[0])

            def layernorm(src, dst, done, sqrt_sem, sqrt_at, ready_sem):
                for t in range(T):
                    last = nc.vector.bn_stats(out=st[:, t, :], in_=src[:, t, :])
                link(last)
                for t in range(T):
                    last = nc.vector.bn_aggr(out=mv[:, t, :], in_=st[:, t, :])
                link(last)
                nc.vector.tensor_scalar(sc2[:, :], mv[:, :, 1], EPS, None, ALU.add).then_inc(ready_sem, 1)
                dve.wait_ge(sqrt_sem, sqrt_at)
                link(nc.vector.reciprocal(rstd[:, :], sc1[:, :]))
                link(nc.vector.tensor_tensor(sc1[:, :], rstd[:, :], rstd[:, :], ALU.mult))
                link(nc.vector.tensor_tensor(sc1[:, :], sc1[:, :], sc2[:, :], ALU.mult))
                link(nc.vector.tensor_scalar(sc1[:, :], sc1[:, :], -0.5, 1.5, ALU.mult, ALU.add))
                link(nc.vector.tensor_tensor(rstd[:, :], rstd[:, :], sc1[:, :], ALU.mult))
                for t in range(T):
                    nc.vector.tensor_scalar(dst[:, t, :], src[:, t, :], mv[:, t, 0:1], rstd[:, t:t + 1],
                                            ALU.subtract, ALU.mult).then_inc(done, 1)

            dve.wait_ge(x_landed, 16)
            layernorm(x_sb, c_sb, c_ready, sqrt_ready, 1, var_ready)
            dve.wait_ge(small_landed, 16 * NSMALL)
            link(nc.vector.tensor_scalar(vecs16[:, :], vecs[:, 0:2], GS, None, ALU.mult))
            nc.vector.tensor_copy(b3r[:, :], b3s[:, :].broadcast_to([3, T])).then_inc(g_ready, 1)
            for h in range(2):
                a, b = h * CH, (h + 1) * CH
                dve.wait_ge(cT_in_psum, h + 1)
                nc.vector.tensor_copy(cT[:, a:b], psT[h][:, :])
                link(nc.vector.tensor_scalar(g32[:, a:b], psT[h][:, :], vecs16[:, 0:1], vecs16[:, 1:2],
                                             ALU.mult, ALU.add))
                link(nc.vector.tensor_copy(gh[:, a:b], g32[:, a:b]))
                nc.vector.tensor_tensor(gl[:, a:b], g32[:, a:b], gh[:, a:b], ALU.subtract).then_inc(g_ready, 1)

            def low_qT(n):
                a, b = cols(n, GR)
                dve.wait_ge(qTh_ready, n + 1)
                nc.vector.tensor_tensor(qTl[:, a:b], stageT[:, a:b], qTh[:, a:b],
                                        ALU.subtract).then_inc(qTl_ready, 1)

            def scores(u, n, has_prev):
                a, b = cols(n, GR)
                dve.wait_ge(scores_in_psum, u * NG + n + 1)
                if has_prev:
                    dve.wait_ge(exp_done, (u - 1) * NG + n + 1)
                    if n == 0:
                        dve.wait_ge(negb_ready, u)
                nc.vector.tensor_scalar(out=S[:, a:b], in0=psS[n % 2][:, 0:b - a], scalar1=1.0 / GS, scalar2=None,
                                        op0=ALU.mult, op1=ALU.max,
                                        accum_out=mxp[:, n:n + 1]).then_inc(scores_out, 1)

            def row_max(u):
                dve.wait_ge(scores_out, (u + 1) * NG)
                nc.vector.tensor_reduce(out=mx[:, bass.ds(u, 1)], in_=mxp[:, :], axis=AX.X,
                                        op=ALU.max).then_inc(max_parts, 1)
                dve.wait_ge(max_parts, u + 1)
                nc.vector.tensor_scalar(negb[:, bass.ds(u, 1)], mx[:, bass.ds(u, 1)], -1.0, LIFT,
                                        ALU.mult, ALU.add).then_inc(negb_ready, 1)

            def low(t, k):
                w = len(tiles(k)) * P
                dve.wait_ge(high_done, t * NT + k + 1)
                nc.vector.tensor_tensor(PTs[:, k % 3, 1, 0:w], psT[k % 3][:, 0:w], PTs[:, k % 3, 0, 0:w],
                                        ALU.subtract).then_inc(low_done, 1)

            def attended(t):
                nc.vector.tensor_reduce(out=Ls[:, :], in_=Lp[:, bass.ds(t * NG, NG)], axis=AX.X,
                                        op=ALU.add).then_inc(o_small, 1)
                dve.wait_ge(o_small, 3 * t + 1)
                nc.vector.reciprocal(Li[:, :], Ls[:, :]).then_inc(o_small, 1)
                dve.wait_ge(o_small, 3 * t + 2)
                dve.wait_ge(pv_done, (t + 1) * NT)
                nc.vector.tensor_scalar(otmp[:, :], psO[:, 0:D], Li[:, :], None, ALU.mult).then_inc(o_small, 1)
                dve.wait_ge(o_small, 3 * t + 3)
                nc.vector.scalar_tensor_tensor(out=a_sb[:, bass.ts(t, D)], in0=psO[:, D:2 * D], scalar=Li[:, :],
                                               in1=otmp[:, :], op0=ALU.mult, op1=ALU.add).then_inc(o_out, 1)

            def step(t, has_next):
                if has_next:
                    scores(t + 1, 0, True)
                    scores(t + 1, 1, True)
                for k in range(NT):
                    low(t, k)
                    if has_next:
                        if k in (2, 4, 6, 8):
                            scores(t + 1, k // 2 + 1, True)
                        if k == 9:
                            scores(t + 1, NG - 1, True)
                            row_max(t + 1)
                attended(t)

            for n in range(NG):
                low_qT(n)
                if n >= 1:
                    scores(0, n - 1, False)
            scores(0, NG - 1, False)
            row_max(0)
            with dve.Fori(0, T - 1) as t:
                step(t, True)
            step(T - 1, False)

            dve.wait_ge(post_pe, 1)
            link(nc.vector.tensor_tensor(Mrow[:, :], mx[:, :], psS[0][:, 0:T], ALU.add))
            nc.vector.tensor_reduce(out=m1[:, :], in_=Mrow[:, :], axis=AX.X, op=ALU.max).then_inc(post_dve, 1)
            dve.wait_ge(post_pe, 2)
            nc.vector.tensor_reduce(out=m2[:, :], in_=psS[1][0:1, 0:P], axis=AX.X, op=ALU.max).then_inc(post_dve, 1)
            dve.wait_ge(post_pe, 3)
            nc.vector.tensor_scalar(nM[:, :], psS[0][:, CH:CH + 1], -1.0, None, ALU.mult).then_inc(post_dve, 1)
            dve.wait_ge(post_pe, 4)
            link(nc.vector.reciprocal(Bi[:, :], psS[1][:, CH:CH + 1]))
            link(nc.vector.tensor_tensor(q2c[:, :], psO[:, 0:1], Bi[:, :], ALU.mult))
            dve.wait_ge(late_landed, 16 * NLATE)
            nc.vector.scalar_tensor_tensor(out=wc2[:, :], in0=wl[:, 3, :], scalar=q2c[:, :], in1=wl[:, 0, :],
                                           op0=ALU.mult, op1=ALU.add).then_inc(post_dve, 1)
            for h in range(2):
                a, b = h * CH, (h + 1) * CH
                dve.wait_ge(post_pe, 5 + h)
                link(nc.vector.tensor_copy(aT[:, a:b], psT[h][:, :]))
                nc.vector.tensor_tensor(caT[:, a:b], aT[:, a:b], cT[:, a:b], ALU.mult).then_inc(post_dve, 1)
            for h in range(2):
                dve.wait_ge(post_pe, 7 + h)
                link(nc.vector.tensor_tensor(x1[:, 4 * h:4 * h + 4, :],
                                             psS[h][:, 0:CH].rearrange("p (t d) -> p t d", d=D),
                                             x_sb[:, 4 * h:4 * h + 4, :], ALU.add))
            layernorm(x1, x2n, post_dve, post_act, 2, post_dve)
            for h in range(2):
                dve.wait_ge(post_pe, 9 + h)
                nc.vector.tensor_copy(x2T[:, h * CH:(h + 1) * CH], psT[h][:, :]).then_inc(post_dve, 1)
            dve.wait_ge(post_pe, 11)
            link(nc.vector.tensor_copy(rsc[:, :, :], psO[:, 0:T * E].rearrange("p (t e) -> p t e", e=E)))
            link(nc.vector.tensor_reduce(out=rmx[:, :], in_=rsc[:, :, :], axis=AX.X, op=ALU.max))
            link(nc.vector.tensor_tensor(cand[:, :, :], rsc[:, :, :],
                                         rmx[:, :].unsqueeze(2).broadcast_to([P, T, E]), ALU.is_lt))
            dve.wait_ge(consts_ready, 4 + E)
            iob = iota_e[:, :].unsqueeze(1).broadcast_to([P, T, E])
            link(nc.vector.tensor_scalar(cand[:, :, :], cand[:, :, :], float(E), None, ALU.mult))
            link(nc.vector.tensor_tensor(cand[:, :, :], cand[:, :, :], iob, ALU.add))
            link(nc.vector.tensor_reduce(out=rmx[:, :], in_=cand[:, :, :], axis=AX.X, op=ALU.min))
            link(nc.vector.tensor_tensor(oneh[:, :, :], iob,
                                         rmx[:, :].unsqueeze(2).broadcast_to([P, T, E]), ALU.is_equal))
            nadd = 0
            for i in range(2 * E):
                e, h = i // 2, i % 2
                dve.wait_ge(y_in_psum, 4 * i + 4)
                for j in range(4):
                    t = 4 * h + j
                    if i >= 2:
                        dve.wait_ge(y_added, 4 * (i - 2) + j + 1)
                    nc.vector.scalar_tensor_tensor(out=x1[:, t, :], in0=psT[i % 2][:, j * D:(j + 1) * D],
                                                   scalar=oneh[:, t, e:e + 1], in1=x1[:, t, :],
                                                   op0=ALU.mult, op1=ALU.add).then_inc(y_added, 1)
            dve.wait_ge(y_added, 8 * E)
            nc.vector.tensor_copy(sc1[:, 0:1], sc2[:, 0:1]).then_inc(y_added, 1)

        @block.tensor
        def _(pe):
            pe.wait_ge(consts_ready, 3)
            for t in range(T):
                pe.wait_ge(c_ready, t + 1)
                last = nc.tensor.transpose(psT[t // 4][:, (t % 4) * P:(t % 4 + 1) * P], c_sb[:, t, :], idf[:, :])
                if t % 4 == 3:
                    last.then_inc(cT_in_psum, 1)

            def scores(u, c, has_prev):
                a, b = cols(c, CH)
                n = c // 2
                if c % 2 == 0:
                    if n >= 2:
                        pe.wait_ge(scores_out, u * NG + n - 1)
                    elif has_prev:
                        pe.wait_ge(scores_out, u * NG)
                dst = psS[n % 2][:, (c % 2) * CH:(c % 2) * CH + b - a]
                g_h, g_l = gh[:, bass.ts(u, P)], gl[:, bass.ts(u, P)]
                nc.tensor.matmul(dst, g_h, qTh[:, a:b], start=True, stop=False)
                nc.tensor.matmul(dst, g_h, qTl[:, a:b], start=False, stop=False)
                last = nc.tensor.matmul(dst, g_l, qTh[:, a:b], start=False, stop=True)
                if c % 2 == 1 or c == NCH - 1:
                    last.then_inc(scores_in_psum, 1)

            def transposes(t, k, has_prev):
                if k % 2 == 0:
                    pe.wait_ge(exp_done, t * NG + k // 2 + 1)
                if k >= 3:
                    pe.wait_ge(low_done, t * NT + k - 2)
                elif has_prev and k == 0:
                    pe.wait_ge(low_done, t * NT)
                for i, j in enumerate(tiles(k)):
                    last = nc.tensor.transpose(psT[k % 3][:, i * P:(i + 1) * P], Pm[:, j * P:(j + 1) * P], idf[:, :])
                last.then_inc(pT_in_psum, 1)

            def weighted(t, k, has_prev):
                pe.wait_ge(low_done, t * NT + k + 1)
                if has_prev and k == 0:
                    pe.wait_ge(o_out, t)
                for i, j in enumerate(tiles(k)):
                    nc.tensor.matmul(psO[:, 0:2 * D], PTs[:, k % 3, 0, i * P:(i + 1) * P],
                                     qn[:, j, :, :].rearrange("p a d -> p (a d)"),
                                     start=(j == 0), stop=False, skip_group_check=True)
                    last = nc.tensor.matmul(psO[:, 0:D], PTs[:, k % 3, 1, i * P:(i + 1) * P], qn[:, j, 0, :],
                                            start=False, stop=(j == QT - 1), skip_group_check=True)
                last.then_inc(pv_done, 1)

            def step(t, has_prev, has_next):
                if has_next:
                    for c in range(4):
                        scores(t + 1, c, True)
                for k in range(NT):
                    transposes(t, k, has_prev)
                    if k >= 1:
                        weighted(t, k - 1, has_prev)
                    if has_next and 4 <= k + 3 < NCH:
                        scores(t + 1, k + 3, True)
                weighted(t, NT - 1, has_prev)

            pe.wait_ge(g_ready, 3)
            for c in range(NCH):
                if c % 2 == 0:
                    pe.wait_ge(qTl_ready, c // 2 + 1)
                scores(0, c, False)
            pe.wait_ge(consts_ready, 4)
            pe.wait_ge(qn_ready, NG)
            step(0, False, True)
            with pe.Fori(1, T - 1) as t:
                step(t, True, True)
            step(T - 1, True, False)

            pe.wait_ge(scores_out, T * NG)
            nc.tensor.matmul(psS[0][:, 0:T], ones[0:3, :], b3r[:, :], start=True, stop=False, skip_group_check=True)
            for t in range(T):
                last = nc.tensor.matmul(psS[0][:, t:t + 1], cT[:, t * P:(t + 1) * P], vecs[:, 2:3],
                                        start=False, stop=(t == T - 1), skip_group_check=True)
            last.then_inc(post_pe, 1)
            pe.wait_ge(post_dve, 1)
            nc.tensor.transpose(psS[1][0:1, 0:P], m1[:, :], idf[:, :]).then_inc(post_pe, 1)
            pe.wait_ge(post_dve, 2)
            nc.tensor.matmul(psS[0][:, CH:CH + 1], ones[0:1, :], m2[:, :], start=True, stop=True).then_inc(post_pe, 1)
            pe.wait_ge(post_act, 1)
            pe.wait_ge(o_out, T)
            for t in range(T):
                nc.tensor.matmul(psO[:, 0:1], c_sb[:, t, :], eb[:, t:t + 1], start=(t == 0), stop=(t == T - 1))
            nc.tensor.matmul(psS[1][:, CH:CH + 1], ones[:, :], es1[:, :], start=True, stop=True).then_inc(post_pe, 1)
            for t in range(T):
                last = nc.tensor.transpose(psT[t // 4][:, (t % 4) * P:(t % 4 + 1) * P], a_sb[:, t * D:(t + 1) * D],
                                           idf[:, :])
                if t % 4 == 3:
                    last.then_inc(post_pe, 1)
            for h in range(2):
                pe.wait_ge(post_dve, 4 + h + 1)
                for j in range(4):
                    t = 4 * h + j
                    dst = psS[h][:, j * D:(j + 1) * D]
                    r = slice(t * P, (t + 1) * P)
                    nc.tensor.matmul(dst, ones[0:1, :], blr[:, :], start=True, stop=False)
                    nc.tensor.matmul(dst, cT[:, r], wc2[:, :], start=False, stop=False)
                    nc.tensor.matmul(dst, aT[:, r], wl[:, 1, :], start=False, stop=False)
                    last = nc.tensor.matmul(dst, caT[:, r], wl[:, 2, :], start=False, stop=True)
                last.then_inc(post_pe, 1)
            base = 7
            for t in range(T):
                pe.wait_ge(post_dve, base + t + 1)
                last = nc.tensor.transpose(psT[t // 4][:, (t % 4) * P:(t % 4 + 1) * P], x2n[:, t, :], idf[:, :])
                if t % 4 == 3:
                    last.then_inc(post_pe, 1)
            pe.wait_ge(post_dve, base + T + 2)
            for t in range(T):
                dst = psO[:, t * E:(t + 1) * E]
                nc.tensor.matmul(dst, ones[0:1, :], brs[:, :], start=True, stop=False)
                last = nc.tensor.matmul(dst, x2T[:, t * P:(t + 1) * P], wrs[:, :], start=False, stop=True)
            last.then_inc(post_pe, 1)

            def down(i):
                e, h = i // 2, i % 2
                pe.wait_ge(gelu_done, (i + 1) * FC)
                if i >= 2:
                    pe.wait_ge(y_added, 4 * (i - 1))
                for j in range(4):
                    dst = psT[i % 2][:, j * D:(j + 1) * D]
                    nc.tensor.matmul(dst, ones[0:1, :], b2s[:, e, :], start=True, stop=False)
                    for f in range(FC):
                        last = nc.tensor.matmul(dst, hT[:, i % 2, f, j * P:(j + 1) * P],
                                                stageN[:, (e * FC + f) * D:(e * FC + f + 1) * D],
                                                start=False, stop=(f == FC - 1))
                    last.then_inc(y_in_psum, 1)

            pe.wait_ge(w1_landed, 16)
            for i in range(2 * E):
                e, h = i // 2, i % 2
                for f in range(FC):
                    if i >= 1:
                        pe.wait_ge(gelu_done, (i - 1) * FC + f + 1)
                    nc.tensor.matmul(bankS[f], stageT[:, e * F + f * P:e * F + (f + 1) * P],
                                     x2T[:, h * CH:(h + 1) * CH], start=True, stop=True).then_inc(h_in_psum, 1)
                if i == 1:
                    pe.wait_ge(w2_landed, 16)
                if i >= 1:
                    down(i - 1)
            down(2 * E - 1)


def kernel(**inputs):
    import numpy as _np
    import concourse.bacc as _bacc
    from concourse import mybir as _mybir
    from concourse.bass_utils import run_bass_kernel_spmd as _run

    a = {k: _np.asarray(v) for k, v in inputs.items()}
    arrays = {
        "in_x": a["x"][0],
        "in_ctxT": a["ctx_1024"][0].T,
        "in_ctx": a["ctx_1024"][0],
        "in_w_cq": a["L0_xattn_w_cq"],
        "in_w_c": a["L0_xattn_w_c"],
        "in_w_q": a["L0_xattn_w_q"],
        "in_b3": _np.stack([a["L0_xattn_b_cq"], a["L0_xattn_b_c"], a["L0_xattn_b_q"]]),
        "in_wlT": a["L0_xattn_W_l"].T,
        "in_b_l": a["L0_xattn_b_l"],
        "in_wr": a["L0_ffn_wr"],
        "in_br": a["L0_ffn_br"],
        "in_w1": a["L0_ffn_w1"],
        "in_b1": a["L0_ffn_b1"].reshape(8, 4, 128).transpose(2, 0, 1).reshape(128, 32),
        "in_w2": a["L0_ffn_w2"],
        "in_b2": a["L0_ffn_b2"],
    }
    arrays = {k: _np.ascontiguousarray(v) for k, v in arrays.items()}
    nc = _bacc.Bacc("TRN2", target_bir_lowering=False, num_devices=1)
    args = [nc.dram_tensor(k, v.shape, _mybir.dt.from_np(v.dtype), kind="ExternalInput").ap()
            for k, v in arrays.items()]
    args.append(nc.dram_tensor("out_x", arrays["in_x"].shape, _mybir.dt.float32, kind="ExternalOutput").ap())
    build(nc, *args)
    r = _run(nc, [arrays], core_ids=[0])
    return r.results[0]["out_x"][None]
```

```python
import concourse.bass as bass
from concourse import mybir
from contextlib import ExitStack
import math

F32 = mybir.dt.float32
F16 = mybir.dt.float16
ACT = mybir.ActivationFunctionType
ALU = mybir.AluOpType
AX = mybir.AxisListType

P = 128


def build(nc, x, ctxT, ctx, w_cq, w_c, w_q, b3, wlT, b_l, wr, br, w1, b1, w2, b2, out):
    N, D = x.shape
    Q = ctx.shape[0]
    E, _, F = w1.shape
    T = N // P
    QT = -(-Q // P)
    QF = Q // P
    QTAIL = Q - QF * P
    QP = QT * P
    FC = F // P
    CH = 512
    NCH = -(-Q // CH)
    GR = 2 * CH
    NG = -(-Q // GR)
    TW = GR // P
    TAILP = QP - (NG - 1) * GR
    GS = 16.0
    LIFT = 14 * math.log(2.0)
    EPS = 1e-5
    LAG = 4

    def cols(k, size):
        return k * size, min((k + 1) * size, Q)

    def tiles(e):
        return range(e * TW, min((e + 1) * TW, QT))

    es = ExitStack()
    with es:
        def sb(name, shape, dt=F32):
            return es.enter_context(nc.sbuf_tensor(name, shape, dt))

        def sem(name):
            return es.enter_context(nc.semaphore(name))

        x_sb = sb("x_sb", [P, T, D])
        c_sb = sb("c_sb", [P, T, D])
        cT = sb("cT", [P, N])
        g32 = sb("g32", [P, N])
        gh = sb("gh", [P, N], F16)
        gl = sb("gl", [P, N], F16)
        stageT = sb("stageT", [P, Q])
        w2f = sb("w2f", [P, E * FC * D])
        qTh = sb("qTh", [P, Q], F16)
        qTl = sb("qTl", [P, Q], F16)
        qn = sb("qn", [P, QT, 2, D], F16)
        S = sb("S", [P, Q])
        Pf = sb("Pf", [P, 3, GR])
        Phl = sb("Phl", [P, 3, 2, GR], F16)
        Ptail = sb("Ptail", [P, 2, TAILP], F16)
        PT = sb("PT", [P, 2 * QT, P], F16)
        a_sb = sb("a_sb", [P, N])
        idf = sb("idf", [P, P])
        ones = sb("ones", [P, P])
        mv = sb("mv", [P, T, 2])
        st = sb("st", [P, T, 6])
        rstd = sb("rstd", [P, T])
        sc1 = sb("sc1", [P, T])
        sc2 = sb("sc2", [P, T])
        mxp = sb("mxp", [P, NG])
        mx = sb("mx", [P, T])
        negb = sb("negb", [P, T])
        Lp = sb("Lp", [P, T * NG])
        Ls = sb("Ls", [P, 1])
        Li = sb("Li", [P, 1])
        otmp = sb("otmp", [P, D])
        vecs = sb("vecs", [P, 4])
        vecs16 = sb("vecs16", [P, 2])
        b3s = sb("b3s", [3, 1])
        b3r = sb("b3r", [3, T])
        wl = sb("wl", [P, 4, D])
        blr = sb("blr", [1, D])
        Mrow = sb("Mrow", [P, T])
        m1 = sb("m1", [P, 1])
        m2 = sb("m2", [1, 1])
        nM = sb("nM", [P, 1])
        eb = sb("eb", [P, T])
        es1 = sb("es1", [P, 1])
        Bi = sb("Bi", [P, 1])
        q2c = sb("q2c", [P, 1])
        wc2 = sb("wc2", [P, D])
        wrs = sb("wrs", [P, E])
        brs = sb("brs", [1, E])
        rsc = sb("rsc", [P, T, E])
        rmx = sb("rmx", [P, T])
        iota_e = sb("iota_e", [P, E])
        cand = sb("cand", [P, T, E])
        oneh = sb("oneh", [P, T, E])
        b1s = sb("b1s", [P, E, FC])
        b2s = sb("b2s", [1, E, D])
        stageN = PT[:, :, :].rearrange("p j c -> p (j c)").bitcast(F32)
        aT, caT = S[:, 0:N], S[:, N:2 * N]
        hT = S[:, 2 * N:2 * N + 2 * FC * CH].rearrange("p (a f n) -> p a f n", a=2, f=FC)
        x1 = Pf[:, 0, :].rearrange("p (t d) -> p t d", d=D)
        x2n = Pf[:, 1, :].rearrange("p (t d) -> p t d", d=D)
        x2T = Pf[:, 2, :]

        psS = [es.enter_context(nc.psum_tensor(f"psS{i}", [P, GR], F32)) for i in range(3)]
        psX = es.enter_context(nc.psum_tensor("psX", [P, CH], F32))
        psT = [psS[2][:, 0:CH], psS[2][:, CH:GR], psX]
        psO = es.enter_context(nc.psum_tensor("psO", [P, CH], F32))
        psA = [psO, psX]
        bankS = [psS[0][:, 0:CH], psS[0][:, CH:GR], psS[1][:, 0:CH], psS[1][:, CH:GR]]

        x_landed = sem("x_landed")
        small_landed = sem("small_landed")
        qT_landed = [sem(f"qT_landed{n}") for n in range(NG)]
        qn_landed = [sem(f"qn_landed{n}") for n in range(NG)]
        qtail_landed = sem("qtail_landed")
        late_landed = sem("late_landed")
        w1_landed = sem("w1_landed")
        w2_landed = sem("w2_landed")
        out_landed = sem("out_landed")
        consts_ready = sem("consts_ready")
        tail_zeroed = sem("tail_zeroed")
        var_ready = sem("var_ready")
        sqrt_ready = sem("sqrt_ready")
        c_ready = sem("c_ready")
        cT_in_psum = sem("cT_in_psum")
        g_ready = sem("g_ready")
        qTh_ready = sem("qTh_ready")
        qTl_ready = sem("qTl_ready")
        qTl_pool_ready = sem("qTl_pool_ready")
        qnh_ready = sem("qnh_ready")
        qn_ready = sem("qn_ready")
        scores_in_psum = sem("scores_in_psum")
        scores_out = sem("scores_out")
        max_parts = sem("max_parts")
        negb_ready = sem("negb_ready")
        exp_done = sem("exp_done")
        pT_landed = [sem(f"pT_landed{e}") for e in range(NG)]
        high_done = sem("high_done")
        low_done = sem("low_done")
        low_pool_done = sem("low_pool_done")
        pv_done = sem("pv_done")
        o_small = sem("o_small")
        o_out = sem("o_out")
        post_pe = sem("post_pe")
        post_dve = sem("post_dve")
        post_act = sem("post_act")
        dve_chain = sem("dve_chain")
        h_in_psum = sem("h_in_psum")
        gelu_done = sem("gelu_done")
        y_in_psum = sem("y_in_psum")
        y_added = sem("y_added")

        block = es.enter_context(nc.Block())

        POOL_LOW = (3, 5)
        DVE_LOW = [n for n in range(NG) if n not in POOL_LOW]

        def ctx_rows(n):
            j0, j1 = n * 8, min(n * 8 + 8, QT)
            return stageN[:, j0 * D:j1 * D].rearrange("p (j d) -> p j d", d=D), j0, j1

        LOW_POOL = (3,)
        LOW_DVE = [e for e in range(NG) if e not in LOW_POOL]

        def wait_low(eng, t, e):
            if e in LOW_POOL:
                eng.wait_ge(low_pool_done, t * len(LOW_POOL) + LOW_POOL.index(e) + 1)
            else:
                eng.wait_ge(low_done, t * len(LOW_DVE) + LOW_DVE.index(e) + 1)

        def piece(e):
            n, w = len(tiles(e)), cols(e, GR)[1] - e * GR
            buf = Phl[:, e % 3, :, :] if e < NG - 1 else Ptail[:, :, :]
            return (buf.rearrange("p a w -> p (a w)"), buf[:, 0, 0:w], buf[:, 1, 0:w],
                    PT[:, 2 * e * TW:2 * e * TW + 2 * n, :])

        @block.sync
        def _(sp):
            sp.dma_start(x_sb[:, :, :], x.rearrange("(t p) d -> p t d", p=P)).then_inc(x_landed, 16)
            for n in range(NG):
                a, b = cols(n, GR)
                sp.dma_start(stageT[:, a:b], ctxT[:, a:b]).then_inc(qT_landed[n], 16)
            for n in range(NG):
                j0, j1 = n * 8, min(n * 8 + 8, QF)
                sp.dma_start(stageN[:, j0 * D:j1 * D].rearrange("p (j d) -> p j d", d=D),
                             ctx[j0 * P:j1 * P, :].rearrange("(j p) d -> p j d", p=P)).then_inc(qn_landed[n], 16)
            sp.wait_ge(tail_zeroed, 1)
            sp.dma_start(stageN[0:QTAIL, QF * D:QT * D], ctx[QF * P:Q, :]).then_inc(qtail_landed, 16)
            sp.dma_start(wl[:, :, :], wlT.rearrange("(k p) o -> p k o", p=P)).then_inc(late_landed, 16)
            sp.wait_ge(qTl_ready, len(DVE_LOW))
            sp.wait_ge(qTl_pool_ready, len(POOL_LOW))
            sp.dma_start(stageT[:, 0:E * F].rearrange("p (e f) -> p e f", f=F),
                         w1.rearrange("e h f -> h e f")).then_inc(w1_landed, 16)
            sp.dma_start(w2f[:, :].rearrange("p (e k d) -> p e k d", k=FC, d=D),
                         w2.rearrange("e (k p) d -> p e k d", p=P)).then_inc(w2_landed, 16)

            def transpose(t, e, has_prev):
                wait_low(sp, t, e)
                if has_prev:
                    sp.wait_ge(pv_done, (t - 1) * NG + e + 1)
                else:
                    sp.wait_ge(qn_ready, e + 1)
                src, _, _, dst = piece(e)
                sp.dma_start_transpose(dst, src).then_inc(pT_landed[e], 16)

            for t in range(T):
                for e in range(NG):
                    transpose(t, e, t > 0)

            sp.wait_ge(y_added, 2 * E * 4 + 1)
            sp.dma_start(out.rearrange("(t p) d -> p t d", p=P), x1[:, :, :]).then_inc(out_landed, 16)
            sp.wait_ge(out_landed, 16)

        NSMALL = 6
        NLATE = 4

        @block.gpsimd
        def _(pool):
            nc.gpsimd.memset(idf[:, :], 0.0).then_inc(consts_ready, 1)
            nc.gpsimd.memset(ones[:, :], 1.0).then_inc(consts_ready, 1)
            pool.wait_ge(consts_ready, 2)
            nc.gpsimd.affine_select(out=idf[:, :], in_=idf[:, :], compare_op=ALU.not_equal, fill=1.0, base=0,
                                    pattern=[[-1, P]], channel_multiplier=1).then_inc(consts_ready, 1)
            nc.gpsimd.memset(stageN[:, QF * D:QT * D], 0.0).then_inc(tail_zeroed, 1)
            nc.gpsimd.memset(Ptail[:, :, :], 0.0).then_inc(consts_ready, 1)
            for e in range(E):
                nc.gpsimd.memset(iota_e[:, e:e + 1], float(e)).then_inc(consts_ready, 1)
            for n in POOL_LOW:
                a, b = cols(n, GR)
                pool.wait_ge(qTh_ready, n + 1)
                nc.gpsimd.tensor_tensor(qTl[:, a:b], stageT[:, a:b], qTh[:, a:b],
                                        ALU.subtract).then_inc(qTl_pool_ready, 1)
            for n in range(NG):
                pool.wait_ge(qnh_ready, n + 1)
                src, j0, j1 = ctx_rows(n)
                nc.gpsimd.tensor_tensor(qn[:, j0:j1, 1, :], src, qn[:, j0:j1, 0, :],
                                        ALU.subtract).then_inc(qn_ready, 1)

            with pool.Fori(0, T) as t:
                for e in LOW_POOL:
                    pool.wait_ge(high_done, t * NG + e + 1)
                    _, hi, lo, _ = piece(e)
                    nc.gpsimd.tensor_tensor(lo, Pf[:, e % 3, 0:hi.shape[1]], hi,
                                            ALU.subtract).then_inc(low_pool_done, 1)

        @block.scalar
        def _(act):
            for i, v in enumerate((w_cq, w_q, w_c)):
                act.dma_start(vecs[:, i:i + 1], v.rearrange("(p o) -> p o", o=1)).then_inc(small_landed, 16)
            act.dma_start(b3s[:, :], b3.rearrange("(p o) -> p o", o=1)).then_inc(small_landed, 16)
            act.dma_start(blr[:, :], b_l.rearrange("(o d) -> o d", o=1)).then_inc(small_landed, 16)
            act.dma_start(brs[:, :], br.rearrange("(o d) -> o d", o=1)).then_inc(small_landed, 16)
            act.dma_start(wrs[:, :], wr).then_inc(late_landed, 16)
            act.dma_start(b2s[:, :, :], b2.rearrange("(o e) d -> o e d", o=1)).then_inc(late_landed, 16)
            act.dma_start(b1s[:, :, :], b1.rearrange("p (e k) -> p e k", k=FC)).then_inc(late_landed, 16)
            act.wait_ge(var_ready, 1)
            nc.scalar.activation(sc1[:, :], sc2[:, :], ACT.Sqrt).then_inc(sqrt_ready, 1)
            for n in range(NG):
                a, b = cols(n, GR)
                act.wait_ge(qT_landed[n], 16)
                nc.scalar.copy(qTh[:, a:b], stageT[:, a:b]).then_inc(qTh_ready, 1)

            for n in range(NG):
                act.wait_ge(qn_landed[n], 16)
                if n == NG - 1:
                    act.wait_ge(qtail_landed, 16)
                src, j0, j1 = ctx_rows(n)
                nc.scalar.copy(qn[:, j0:j1, 0, :], src).then_inc(qnh_ready, 1)

            def exp_piece(t, e):
                a, b = cols(e, GR)
                if e == 0:
                    act.wait_ge(negb_ready, t + 1)
                if e >= 3:
                    wait_low(act, t, e - 3)
                elif not isinstance(t, int):
                    wait_low(act, t - 1, (NG - 1, 4, 5)[e])
                nc.scalar.activation(Pf[:, e % 3, 0:b - a], S[:, a:b], ACT.Exp, bias=negb[:, bass.ds(t, 1)],
                                     accum_out=Lp[:, bass.ds(t * NG + e, 1)]).then_inc(exp_done, 1)

            def high(t, e, has_prev):
                act.wait_ge(exp_done, t * NG + e + 1)
                if e == NG - 1 and has_prev:
                    act.wait_ge(pT_landed[e], 16 * t)
                elif e == NG - 1:
                    act.wait_ge(consts_ready, 4)
                elif e >= 3:
                    act.wait_ge(pT_landed[e - 3], 16 * (t + 1))
                elif has_prev:
                    act.wait_ge(pT_landed[e + 3], 16 * t)
                _, hi, _, _ = piece(e)
                nc.scalar.copy(hi, Pf[:, e % 3, 0:hi.shape[1]]).then_inc(high_done, 1)

            def step(t, has_prev):
                for e in range(NG):
                    exp_piece(t, e)
                    high(t, e, has_prev)

            step(0, False)
            with act.Fori(1, T) as t:
                step(t, True)
            act.wait_ge(post_dve, 3)
            nc.scalar.activation(eb[:, :], Mrow[:, :], ACT.Exp, bias=nM[:, :],
                                 accum_out=es1[:, :]).then_inc(post_act, 1)
            act.wait_ge(post_dve, 7)
            nc.scalar.activation(sc1[:, :], sc2[:, :], ACT.Sqrt).then_inc(post_act, 1)
            act.wait_ge(late_landed, 16 * NLATE)
            for i in range(2 * E):
                e, h = i // 2, i % 2
                for f in range(FC):
                    act.wait_ge(h_in_psum, i * FC + f + 1)
                    if i >= 2 and f == 0:
                        act.wait_ge(y_in_psum, (i - 1) * 4)
                    nc.scalar.activation(hT[:, i % 2, f, :], bankS[f], ACT.Gelu,
                                         bias=b1s[:, e, f:f + 1]).then_inc(gelu_done, 1)

        @block.vector
        def _(dve):
            chain = [0]

            def link(ins):
                chain[0] += 1
                ins.then_inc(dve_chain, 1)
                dve.wait_ge(dve_chain, chain[0])

            def layernorm(src, dst, done, sqrt_sem, sqrt_at, ready_sem):
                for t in range(T):
                    last = nc.vector.bn_stats(out=st[:, t, :], in_=src[:, t, :])
                link(last)
                for t in range(T):
                    last = nc.vector.bn_aggr(out=mv[:, t, :], in_=st[:, t, :])
                link(last)
                nc.vector.tensor_scalar(sc2[:, :], mv[:, :, 1], EPS, None, ALU.add).then_inc(ready_sem, 1)
                dve.wait_ge(sqrt_sem, sqrt_at)
                link(nc.vector.reciprocal(rstd[:, :], sc1[:, :]))
                link(nc.vector.tensor_tensor(sc1[:, :], rstd[:, :], rstd[:, :], ALU.mult))
                link(nc.vector.tensor_tensor(sc1[:, :], sc1[:, :], sc2[:, :], ALU.mult))
                link(nc.vector.tensor_scalar(sc1[:, :], sc1[:, :], -0.5, 1.5, ALU.mult, ALU.add))
                link(nc.vector.tensor_tensor(rstd[:, :], rstd[:, :], sc1[:, :], ALU.mult))
                for t in range(T):
                    nc.vector.tensor_scalar(dst[:, t, :], src[:, t, :], mv[:, t, 0:1], rstd[:, t:t + 1],
                                            ALU.subtract, ALU.mult).then_inc(done, 1)

            dve.wait_ge(x_landed, 16)
            layernorm(x_sb, c_sb, c_ready, sqrt_ready, 1, var_ready)
            dve.wait_ge(small_landed, 16 * NSMALL)
            link(nc.vector.tensor_scalar(vecs16[:, :], vecs[:, 0:2], GS, None, ALU.mult))
            nc.vector.tensor_copy(b3r[:, :], b3s[:, :].broadcast_to([3, T])).then_inc(g_ready, 1)
            for h in range(2):
                a, b = h * CH, (h + 1) * CH
                dve.wait_ge(cT_in_psum, h + 1)
                nc.vector.tensor_copy(cT[:, a:b], psT[h][:, :])
                link(nc.vector.tensor_scalar(g32[:, a:b], psT[h][:, :], vecs16[:, 0:1], vecs16[:, 1:2],
                                             ALU.mult, ALU.add))
                link(nc.vector.tensor_copy(gh[:, a:b], g32[:, a:b]))
                nc.vector.tensor_tensor(gl[:, a:b], g32[:, a:b], gh[:, a:b], ALU.subtract).then_inc(g_ready, 1)

            def low_qT(n):
                a, b = cols(n, GR)
                dve.wait_ge(qTh_ready, n + 1)
                nc.vector.tensor_tensor(qTl[:, a:b], stageT[:, a:b], qTh[:, a:b],
                                        ALU.subtract).then_inc(qTl_ready, 1)

            def scores(u, n, has_prev):
                a, b = cols(n, GR)
                dve.wait_ge(scores_in_psum, u * NG + n + 1)
                if has_prev:
                    dve.wait_ge(exp_done, (u - 1) * NG + n + 1)
                    if n == 0:
                        dve.wait_ge(negb_ready, u)
                nc.vector.tensor_scalar(out=S[:, a:b], in0=psS[n % 3][:, 0:b - a], scalar1=1.0 / GS, scalar2=None,
                                        op0=ALU.mult, op1=ALU.max,
                                        accum_out=mxp[:, n:n + 1]).then_inc(scores_out, 1)

            def row_max(u):
                dve.wait_ge(scores_out, (u + 1) * NG)
                nc.vector.tensor_reduce(out=mx[:, bass.ds(u, 1)], in_=mxp[:, :], axis=AX.X,
                                        op=ALU.max).then_inc(max_parts, 1)
                dve.wait_ge(max_parts, u + 1)
                nc.vector.tensor_scalar(negb[:, bass.ds(u, 1)], mx[:, bass.ds(u, 1)], -1.0, LIFT,
                                        ALU.mult, ALU.add).then_inc(negb_ready, 1)

            def low(t, e):
                if e in LOW_POOL:
                    return
                dve.wait_ge(high_done, t * NG + e + 1)
                _, hi, lo, _ = piece(e)
                nc.vector.tensor_tensor(lo, Pf[:, e % 3, 0:hi.shape[1]], hi, ALU.subtract).then_inc(low_done, 1)

            def attended(t, odd):
                nc.vector.tensor_reduce(out=Ls[:, :], in_=Lp[:, bass.ds(t * NG, NG)], axis=AX.X,
                                        op=ALU.add).then_inc(o_small, 1)
                dve.wait_ge(o_small, 3 * t + 1)
                nc.vector.reciprocal(Li[:, :], Ls[:, :]).then_inc(o_small, 1)
                dve.wait_ge(o_small, 3 * t + 2)
                dve.wait_ge(pv_done, (t + 1) * NG)
                nc.vector.tensor_scalar(otmp[:, :], psA[odd][:, 0:D], Li[:, :], None, ALU.mult).then_inc(o_small, 1)
                dve.wait_ge(o_small, 3 * t + 3)
                nc.vector.scalar_tensor_tensor(out=a_sb[:, bass.ts(t, D)], in0=psA[odd][:, D:2 * D], scalar=Li[:, :],
                                               in1=otmp[:, :], op0=ALU.mult, op1=ALU.add).then_inc(o_out, 1)

            def step(t, odd, has_prev, has_next):
                for e in range(NG):
                    if e == LAG and has_prev:
                        attended(t - 1, 1 - odd)
                    if has_next:
                        scores(t + 1, e, True)
                    low(t, e)
                if has_next:
                    row_max(t + 1)

            for n in range(NG):
                if n in DVE_LOW:
                    low_qT(n)
                if n >= 1:
                    scores(0, n - 1, False)
            scores(0, NG - 1, False)
            row_max(0)
            step(0, 0, False, True)
            with dve.Fori(1, T - 2, 2) as t:
                step(t, 1, True, True)
                step(t + 1, 0, True, True)
            step(T - 1, 1, True, False)
            attended(T - 1, 1)

            dve.wait_ge(post_pe, 1)
            link(nc.vector.tensor_tensor(Mrow[:, :], mx[:, :], psS[0][:, 0:T], ALU.add))
            nc.vector.tensor_reduce(out=m1[:, :], in_=Mrow[:, :], axis=AX.X, op=ALU.max).then_inc(post_dve, 1)
            dve.wait_ge(post_pe, 2)
            nc.vector.tensor_reduce(out=m2[:, :], in_=psS[1][0:1, 0:P], axis=AX.X, op=ALU.max).then_inc(post_dve, 1)
            dve.wait_ge(post_pe, 3)
            nc.vector.tensor_scalar(nM[:, :], psS[0][:, CH:CH + 1], -1.0, None, ALU.mult).then_inc(post_dve, 1)
            dve.wait_ge(post_pe, 4)
            link(nc.vector.reciprocal(Bi[:, :], psS[1][:, CH:CH + 1]))
            link(nc.vector.tensor_tensor(q2c[:, :], psO[:, 0:1], Bi[:, :], ALU.mult))
            dve.wait_ge(late_landed, 16 * NLATE)
            nc.vector.scalar_tensor_tensor(out=wc2[:, :], in0=wl[:, 3, :], scalar=q2c[:, :], in1=wl[:, 0, :],
                                           op0=ALU.mult, op1=ALU.add).then_inc(post_dve, 1)
            for h in range(2):
                a, b = h * CH, (h + 1) * CH
                dve.wait_ge(post_pe, 5 + h)
                link(nc.vector.tensor_copy(aT[:, a:b], psT[h][:, :]))
                nc.vector.tensor_tensor(caT[:, a:b], aT[:, a:b], cT[:, a:b], ALU.mult).then_inc(post_dve, 1)
            for h in range(2):
                dve.wait_ge(post_pe, 7 + h)
                link(nc.vector.tensor_tensor(x1[:, 4 * h:4 * h + 4, :],
                                             psS[h][:, 0:CH].rearrange("p (t d) -> p t d", d=D),
                                             x_sb[:, 4 * h:4 * h + 4, :], ALU.add))
            layernorm(x1, x2n, post_dve, post_act, 2, post_dve)
            for h in range(2):
                dve.wait_ge(post_pe, 9 + h)
                nc.vector.tensor_copy(x2T[:, h * CH:(h + 1) * CH], psT[h][:, :]).then_inc(post_dve, 1)
            dve.wait_ge(post_pe, 11)
            link(nc.vector.tensor_copy(rsc[:, :, :], psO[:, 0:T * E].rearrange("p (t e) -> p t e", e=E)))
            link(nc.vector.tensor_reduce(out=rmx[:, :], in_=rsc[:, :, :], axis=AX.X, op=ALU.max))
            link(nc.vector.tensor_tensor(cand[:, :, :], rsc[:, :, :],
                                         rmx[:, :].unsqueeze(2).broadcast_to([P, T, E]), ALU.is_lt))
            dve.wait_ge(consts_ready, 4 + E)
            iob = iota_e[:, :].unsqueeze(1).broadcast_to([P, T, E])
            link(nc.vector.tensor_scalar(cand[:, :, :], cand[:, :, :], float(E), None, ALU.mult))
            link(nc.vector.tensor_tensor(cand[:, :, :], cand[:, :, :], iob, ALU.add))
            link(nc.vector.tensor_reduce(out=rmx[:, :], in_=cand[:, :, :], axis=AX.X, op=ALU.min))
            link(nc.vector.tensor_tensor(oneh[:, :, :], iob,
                                         rmx[:, :].unsqueeze(2).broadcast_to([P, T, E]), ALU.is_equal))
            nadd = 0
            for i in range(2 * E):
                e, h = i // 2, i % 2
                dve.wait_ge(y_in_psum, 4 * i + 4)
                for j in range(4):
                    t = 4 * h + j
                    if i >= 2:
                        dve.wait_ge(y_added, 4 * (i - 2) + j + 1)
                    nc.vector.scalar_tensor_tensor(out=x1[:, t, :], in0=psT[i % 2][:, j * D:(j + 1) * D],
                                                   scalar=oneh[:, t, e:e + 1], in1=x1[:, t, :],
                                                   op0=ALU.mult, op1=ALU.add).then_inc(y_added, 1)
            dve.wait_ge(y_added, 8 * E)
            nc.vector.tensor_copy(sc1[:, 0:1], sc2[:, 0:1]).then_inc(y_added, 1)

        @block.tensor
        def _(pe):
            pe.wait_ge(consts_ready, 3)
            for t in range(T):
                pe.wait_ge(c_ready, t + 1)
                last = nc.tensor.transpose(psT[t // 4][:, (t % 4) * P:(t % 4 + 1) * P], c_sb[:, t, :], idf[:, :])
                if t % 4 == 3:
                    last.then_inc(cT_in_psum, 1)

            def scores(u, c, has_prev):
                a, b = cols(c, CH)
                n = c // 2
                if c % 2 == 0:
                    if n >= 3:
                        pe.wait_ge(scores_out, u * NG + n - 2)
                    elif has_prev and n == 0:
                        pe.wait_ge(scores_out, u * NG)
                dst = psS[n % 3][:, (c % 2) * CH:(c % 2) * CH + b - a]
                g_h, g_l = gh[:, bass.ts(u, P)], gl[:, bass.ts(u, P)]
                nc.tensor.matmul(dst, g_h, qTh[:, a:b], start=True, stop=False)
                nc.tensor.matmul(dst, g_h, qTl[:, a:b], start=False, stop=False)
                last = nc.tensor.matmul(dst, g_l, qTh[:, a:b], start=False, stop=True)
                if c % 2 == 1 or c == NCH - 1:
                    last.then_inc(scores_in_psum, 1)

            def weighted(t, odd, e, has_prev):
                pe.wait_ge(pT_landed[e], 16 * (t + 1))
                if not has_prev:
                    pe.wait_ge(qn_ready, e + 1)
                if has_prev and e == 0 and (not isinstance(t, int) or t > 1):
                    pe.wait_ge(o_out, t - 1)
                n = len(tiles(e))
                for i, j in enumerate(tiles(e)):
                    nc.tensor.matmul(psA[odd][:, 0:2 * D], PT[:, 2 * e * TW + i, :],
                                     qn[:, j, :, :].rearrange("p a d -> p (a d)"),
                                     start=(j == 0), stop=False, skip_group_check=True)
                    last = nc.tensor.matmul(psA[odd][:, 0:D], PT[:, 2 * e * TW + n + i, :], qn[:, j, 0, :],
                                            start=False, stop=(j == QT - 1), skip_group_check=True)
                last.then_inc(pv_done, 1)

            def step(t, odd, has_prev, has_next):
                for e in range(NG):
                    if has_next:
                        for c in range(2 * e, min(2 * e + 2, NCH)):
                            scores(t + 1, c, True)
                    if e >= LAG:
                        weighted(t, odd, e - LAG, has_prev)
                    elif has_prev:
                        weighted(t - 1, 1 - odd, NG - LAG + e, True)

            pe.wait_ge(g_ready, 3)
            for c in range(NCH):
                if c % 2 == 0 and c // 2 in DVE_LOW:
                    pe.wait_ge(qTl_ready, DVE_LOW.index(c // 2) + 1)
                elif c % 2 == 0:
                    pe.wait_ge(qTl_pool_ready, POOL_LOW.index(c // 2) + 1)
                scores(0, c, False)
            step(0, 0, False, True)
            pe.wait_ge(qn_ready, NG)
            with pe.Fori(1, T - 2, 2) as t:
                step(t, 1, True, True)
                step(t + 1, 0, True, True)
            step(T - 1, 1, True, False)
            for e in range(NG - LAG, NG):
                weighted(T - 1, 1, e, True)

            pe.wait_ge(scores_out, T * NG)
            nc.tensor.matmul(psS[0][:, 0:T], ones[0:3, :], b3r[:, :], start=True, stop=False, skip_group_check=True)
            for t in range(T):
                last = nc.tensor.matmul(psS[0][:, t:t + 1], cT[:, t * P:(t + 1) * P], vecs[:, 2:3],
                                        start=False, stop=(t == T - 1), skip_group_check=True)
            last.then_inc(post_pe, 1)
            pe.wait_ge(post_dve, 1)
            nc.tensor.transpose(psS[1][0:1, 0:P], m1[:, :], idf[:, :]).then_inc(post_pe, 1)
            pe.wait_ge(post_dve, 2)
            nc.tensor.matmul(psS[0][:, CH:CH + 1], ones[0:1, :], m2[:, :], start=True, stop=True).then_inc(post_pe, 1)
            pe.wait_ge(post_act, 1)
            pe.wait_ge(o_out, T)
            for t in range(T):
                nc.tensor.matmul(psO[:, 0:1], c_sb[:, t, :], eb[:, t:t + 1], start=(t == 0), stop=(t == T - 1))
            nc.tensor.matmul(psS[1][:, CH:CH + 1], ones[:, :], es1[:, :], start=True, stop=True).then_inc(post_pe, 1)
            for t in range(T):
                last = nc.tensor.transpose(psT[t // 4][:, (t % 4) * P:(t % 4 + 1) * P], a_sb[:, t * D:(t + 1) * D],
                                           idf[:, :])
                if t % 4 == 3:
                    last.then_inc(post_pe, 1)
            for h in range(2):
                pe.wait_ge(post_dve, 4 + h + 1)
                for j in range(4):
                    t = 4 * h + j
                    dst = psS[h][:, j * D:(j + 1) * D]
                    r = slice(t * P, (t + 1) * P)
                    nc.tensor.matmul(dst, ones[0:1, :], blr[:, :], start=True, stop=False)
                    nc.tensor.matmul(dst, cT[:, r], wc2[:, :], start=False, stop=False)
                    nc.tensor.matmul(dst, aT[:, r], wl[:, 1, :], start=False, stop=False)
                    last = nc.tensor.matmul(dst, caT[:, r], wl[:, 2, :], start=False, stop=True)
                last.then_inc(post_pe, 1)
            base = 7
            for t in range(T):
                pe.wait_ge(post_dve, base + t + 1)
                last = nc.tensor.transpose(psT[t // 4][:, (t % 4) * P:(t % 4 + 1) * P], x2n[:, t, :], idf[:, :])
                if t % 4 == 3:
                    last.then_inc(post_pe, 1)
            pe.wait_ge(post_dve, base + T + 2)
            for t in range(T):
                dst = psO[:, t * E:(t + 1) * E]
                nc.tensor.matmul(dst, ones[0:1, :], brs[:, :], start=True, stop=False)
                last = nc.tensor.matmul(dst, x2T[:, t * P:(t + 1) * P], wrs[:, :], start=False, stop=True)
            last.then_inc(post_pe, 1)

            def down(i):
                e, h = i // 2, i % 2
                pe.wait_ge(gelu_done, (i + 1) * FC)
                if i >= 2:
                    pe.wait_ge(y_added, 4 * (i - 1))
                for j in range(4):
                    dst = psT[i % 2][:, j * D:(j + 1) * D]
                    nc.tensor.matmul(dst, ones[0:1, :], b2s[:, e, :], start=True, stop=False)
                    for f in range(FC):
                        last = nc.tensor.matmul(dst, hT[:, i % 2, f, j * P:(j + 1) * P],
                                                w2f[:, (e * FC + f) * D:(e * FC + f + 1) * D],
                                                start=False, stop=(f == FC - 1))
                    last.then_inc(y_in_psum, 1)

            pe.wait_ge(w1_landed, 16)
            for i in range(2 * E):
                e, h = i // 2, i % 2
                for f in range(FC):
                    if i >= 1:
                        pe.wait_ge(gelu_done, (i - 1) * FC + f + 1)
                    nc.tensor.matmul(bankS[f], stageT[:, e * F + f * P:e * F + (f + 1) * P],
                                     x2T[:, h * CH:(h + 1) * CH], start=True, stop=True).then_inc(h_in_psum, 1)
                if i == 1:
                    pe.wait_ge(w2_landed, 16)
                if i >= 1:
                    down(i - 1)
            down(2 * E - 1)


def kernel(**inputs):
    import numpy as _np
    import concourse.bacc as _bacc
    from concourse import mybir as _mybir
    from concourse.bass_utils import run_bass_kernel_spmd as _run

    a = {k: _np.asarray(v) for k, v in inputs.items()}
    arrays = {
        "in_x": a["x"][0],
        "in_ctxT": a["ctx_1024"][0].T,
        "in_ctx": a["ctx_1024"][0],
        "in_w_cq": a["L0_xattn_w_cq"],
        "in_w_c": a["L0_xattn_w_c"],
        "in_w_q": a["L0_xattn_w_q"],
        "in_b3": _np.stack([a["L0_xattn_b_cq"], a["L0_xattn_b_c"], a["L0_xattn_b_q"]]),
        "in_wlT": a["L0_xattn_W_l"].T,
        "in_b_l": a["L0_xattn_b_l"],
        "in_wr": a["L0_ffn_wr"],
        "in_br": a["L0_ffn_br"],
        "in_w1": a["L0_ffn_w1"],
        "in_b1": a["L0_ffn_b1"].reshape(8, 4, 128).transpose(2, 0, 1).reshape(128, 32),
        "in_w2": a["L0_ffn_w2"],
        "in_b2": a["L0_ffn_b2"],
    }
    arrays = {k: _np.ascontiguousarray(v) for k, v in arrays.items()}
    nc = _bacc.Bacc("TRN2", target_bir_lowering=False, num_devices=1)
    args = [nc.dram_tensor(k, v.shape, _mybir.dt.from_np(v.dtype), kind="ExternalInput").ap()
            for k, v in arrays.items()]
    args.append(nc.dram_tensor("out_x", arrays["in_x"].shape, _mybir.dt.float32, kind="ExternalOutput").ap())
    build(nc, *args)
    r = _run(nc, [arrays], core_ids=[0])
    return r.results[0]["out_x"][None]
```

```python
import concourse.bass as bass
from concourse import mybir
from contextlib import ExitStack
import math

F32 = mybir.dt.float32
F16 = mybir.dt.float16
I32 = mybir.dt.int32
ACT = mybir.ActivationFunctionType
ALU = mybir.AluOpType
AX = mybir.AxisListType

P = 128


def build(nc, x, ctxT, ctx, w3, b3, wlT, b_l, wr, br, w1, b1, w2, b2, out):
    N, D = x.shape
    Q = ctx.shape[0]
    E, _, F = w1.shape
    T = N // P
    QT = -(-Q // P)
    QF = Q // P
    QTAIL = Q - QF * P
    QP = QT * P
    FC = F // P
    CH = 512
    NCH = -(-Q // CH)
    GR = 2 * CH
    NG = -(-Q // GR)
    TW = GR // P
    TAILP = QP - (NG - 1) * GR
    GS = 16.0
    LIFT = 14 * math.log(2.0)
    EPS = 1e-5
    WC = E * F // (T // 2)
    NB = T + E - 1
    ROUTE_CONSTS = 17
    NSMALL, NLATE = 2, 4
    ROW = 2 * D + 1
    NOWHERE = 1 << 20
    RING = 3
    XRE = E * F + (F + D) + (F + D) // 2
    LAG = 4

    def cols(k, size):
        return k * size, min((k + 1) * size, Q)

    def tiles(e):
        return range(e * TW, min((e + 1) * TW, QT))

    es = ExitStack()
    with es:
        def sb(name, shape, dt=F32):
            return es.enter_context(nc.sbuf_tensor(name, shape, dt))

        def sem(name):
            return es.enter_context(nc.semaphore(name))

        c_sb = sb("c_sb", [P, T, D])
        cT = sb("cT", [P, N])
        gh = sb("gh", [P, N], F16)
        gl = sb("gl", [P, N], F16)
        stageT = sb("stageT", [P, Q])
        w1p = sb("w1p", [P, 2, E * F], F16)
        w2p = sb("w2p", [P, 2, E * F], F16)
        qTh = sb("qTh", [P, Q], F16)
        qTl = sb("qTl", [P, Q], F16)
        qn = sb("qn", [P, QT, 2, D], F16)
        S = sb("S", [P, Q])
        Pf = sb("Pf", [P, 3, GR])
        Phl = sb("Phl", [P, 3, 2, GR], F16)
        Ptail = sb("Ptail", [P, 2, TAILP], F16)
        PT = sb("PT", [P, 2 * QT, P], F16)
        a_sb = sb("a_sb", [P, N])
        g32 = a_sb
        idf = sb("idf", [P, P])
        ones = sb("ones", [P, P])
        mv = sb("mv", [P, T, 2])
        st = sb("st", [P, T, 6])
        rstd = sb("rstd", [P, T])
        sc1 = sb("sc1", [P, T])
        sc2 = sb("sc2", [P, T])
        mxp = sb("mxp", [P, NG])
        mx = sb("mx", [P, T])
        negb = sb("negb", [P, T])
        Lp = sb("Lp", [P, T * NG])
        Ls = sb("Ls", [P, 1])
        Li = sb("Li", [P, 1])
        otmp = sb("otmp", [P, D])
        vecs = sb("vecs", [P, 4])
        vecs16 = sb("vecs16", [P, 2])
        b3s = sb("b3s", [3, 1])
        b3r = sb("b3r", [3, T])
        wl = sb("wl", [P, 4, D])
        blr = sb("blr", [P, D])
        row_term = sb("row_term", [P, T])
        Mrow = sb("Mrow", [P, T])
        m1 = sb("m1", [P, 1])
        m2 = sb("m2", [1, 1])
        nM = sb("nM", [P, 1])
        eb = sb("eb", [P, T])
        es1 = sb("es1", [P, 1])
        warm = sb("warm", [P, 3])
        Bi = sb("Bi", [P, 1])
        q2c = sb("q2c", [P, 1])
        wc2 = sb("wc2", [P, D])
        wrs = sb("wrs", [P, E])
        brs = sb("brs", [P, E])
        stageN = PT[:, :, :].rearrange("p j c -> p (j c)").bitcast(F32)
        x_re = stageT[:, XRE:XRE + N].rearrange("p (t d) -> p t d", d=D)
        b12 = stageT[:, XRE + N:XRE + N + (F + D) // 2].bitcast(F16)
        pick = stageT[:, E * F:E * F + E * P // 2].bitcast(F16).rearrange("p (e w) -> p e w", w=P)
        empty = stageT[:, E * F + E * P // 2:E * F + E * P // 2 + ROW]
        before = sb("before", [P, P], F16)
        ones16 = sb("ones16", [P, P], F16)
        iota_e = sb("iota_e", [P, E])
        ints = sb("ints", [P, NB * E], I32)
        kedge = sb("kedge", [P, E, T])
        slot_no = sb("slot_no", [P, NB, E])
        tri = sb("tri", [P, E, E])
        token = sb("token", [P, T], I32)
        ids = sb("ids", [P, RING], I32)
        aT, caT = qTh[:, 0:2 * N].bitcast(F32), qTh[:, 2 * N:4 * N].bitcast(F32)
        pay = qTl[:, 0:2 * T * ROW].bitcast(F32).rearrange("p (t w) -> p t w", w=ROW)
        at = [0]

        def carve(n, dt=F32):
            at[0] += n
            return S[:, at[0] - n:at[0]].bitcast(dt) if dt != F32 else S[:, at[0] - n:at[0]]

        xblk = carve(RING * D).rearrange("p (r d) -> p r d", d=D)
        rest = carve(NB * (D + 1)).rearrange("p (b w) -> p b w", w=D + 1)
        hf = carve(RING * F).rearrange("p (r f) -> p r f", f=F)
        more = carve(E * T).rearrange("p (a b) -> p a b", b=T)
        rank = carve(T * E).rearrange("p (a b) -> p a b", b=E)
        rsc = carve(T * E).rearrange("p (a b) -> p a b", b=E)
        cand = carve(T * E).rearrange("p (a b) -> p a b", b=E)
        past = carve(NB * E).rearrange("p (a b) -> p a b", b=E)
        oneh = carve(T * E // 2, F16).rearrange("p (a b) -> p a b", b=E)
        nblk, sblk, eblk = carve(E), carve(E), carve(E)
        posf, rmx, bexpf = carve(T), carve(T), carve(NB)
        pos, bexp = carve(T, I32), carve(NB, I32)
        parts_ring = Phl[:, :, :, :].rearrange("p r a w -> p (r a w)")
        hp = parts_ring[:, 0:RING * 2 * F].rearrange("p (r a f) -> p r a f", r=RING, a=2)
        xTp = parts_ring[:, RING * 2 * F:RING * 2 * F + RING * 2 * P].rearrange("p (r a w) -> p r a w", r=RING, a=2)
        x2n = pay[:, :, 0:D]
        x1 = pay[:, :, D:2 * D]
        x2T = Pf[:, 0, 0:N]
        yf = stageT[:, 0:RING * D].rearrange("p (r d) -> p r d", d=D)
        yt = stageT[:, RING * D:2 * RING * D].rearrange("p (r d) -> p r d", d=D)
        x_sb = Pf[:, 0, :].rearrange("p (t d) -> p t d", d=D)
        b12f = stageT[0:40, E * F:E * F + F + D]
        b12t = stageT[0:40, E * F + F + D:E * F + F + D + (F + D) // 2].bitcast(F16)

        psS = [es.enter_context(nc.psum_tensor(f"psS{i}", [P, GR], F32)) for i in range(3)]
        psX = es.enter_context(nc.psum_tensor("psX", [P, CH], F32))
        psO = es.enter_context(nc.psum_tensor("psO", [P, CH], F32))
        psA = [psO, psX]

        x_landed = sem("x_landed")
        x_re_landed = sem("x_re_landed")
        x_re_ready = sem("x_re_ready")
        small_landed = sem("small_landed")
        qT_landed = [sem(f"qT_landed{n}") for n in range(NG)]
        qn_landed = [sem(f"qn_landed{n}") for n in range(NG)]
        qtail_landed = sem("qtail_landed")
        late_landed = sem("late_landed")
        w_landed = [sem(f"w_landed{k}") for k in range(T)]
        consts_ready = sem("consts_ready")
        tail_zeroed = sem("tail_zeroed")
        var_ready = sem("var_ready")
        sqrt_ready = sem("sqrt_ready")
        c_ready = sem("c_ready")
        cT_in_psum = sem("cT_in_psum")
        g_ready = sem("g_ready")
        vecs16_ready = sem("vecs16_ready")
        cT_ready = sem("cT_ready")
        late_g_ready = sem("late_g_ready")
        late_gh_ready = sem("late_gh_ready")
        late_gl_ready = sem("late_gl_ready")
        qTh_ready = sem("qTh_ready")
        qTl_ready = sem("qTl_ready")
        qTl_pool_ready = sem("qTl_pool_ready")
        qnh_ready = sem("qnh_ready")
        qn_ready = sem("qn_ready")
        scores_in_psum = sem("scores_in_psum")
        scores_out = sem("scores_out")
        max_parts = sem("max_parts")
        negb_ready = sem("negb_ready")
        exp_done = sem("exp_done")
        pT_landed = [sem(f"pT_landed{e}") for e in range(NG)]
        high_done = sem("high_done")
        low_done = sem("low_done")
        low_pool_done = sem("low_pool_done")
        pv_done = sem("pv_done")
        o_small = sem("o_small")
        o_out = sem("o_out")
        row_term_in_psum = sem("row_term_in_psum")
        row_term_ready = sem("row_term_ready")
        m1_ready = sem("m1_ready")
        m1T_in_psum = sem("m1T_in_psum")
        m2_ready = sem("m2_ready")
        top_in_psum = sem("top_in_psum")
        nM_ready = sem("nM_ready")
        eb_ready = sem("eb_ready")
        q2c_in_psum = sem("q2c_in_psum")
        wc2_ready = sem("wc2_ready")
        aT_in_psum = sem("aT_in_psum")
        caT_ready = sem("caT_ready")
        z_in_psum = sem("z_in_psum")
        x2n_ready = sem("x2n_ready")
        x2T_in_psum = sem("x2T_in_psum")
        x2T_ready = sem("x2T_ready")
        router_in_psum = sem("router_in_psum")
        chosen_ready = sem("chosen_ready")
        ranks_in_psum = sem("ranks_in_psum")
        dve_chain = sem("dve_chain")
        route_consts = sem("route_consts")
        w_high = sem("w_high")
        w_low = sem("w_low")
        b12_landed = sem("b12_landed")
        b12_ready = sem("b12_ready")
        empty_ready = sem("empty_ready")
        slots_emptied = sem("slots_emptied")
        tokens_ready = sem("tokens_ready")
        experts_ready = sem("experts_ready")
        pos_ready = sem("pos_ready")
        rows_sent = sem("rows_sent")
        x_blk_landed = [sem(f"x_blk_landed{i}") for i in range(RING)]
        rest_landed = sem("rest_landed")
        xT_in_psum = sem("xT_in_psum")
        xT_high = sem("xT_high")
        xT_low = sem("xT_low")
        h_in_psum = sem("h_in_psum")
        gelu_done = sem("gelu_done")
        h_high = sem("h_high")
        h_low = sem("h_low")
        y_in_psum = sem("y_in_psum")
        y_part = sem("y_part")
        y_ready = sem("y_ready")
        y_landed = [sem(f"y_landed{i}") for i in range(RING)]

        xs = nc.dram_tensor("rows_by_expert", [NB * P, ROW], F32).ap()

        block = es.enter_context(nc.Block())

        psH = [psS[i][:, 0:CH] for i in range(RING)]
        psY = [psS[i][:, CH:CH + 2 * D] for i in range(RING)]
        psXT = [psX, psO, psX]

        H = T // 2
        GROUPS = ((0, H), (H, T - 1), (T - 1, T))
        TURNS = ((0, H), (H, T - 2), (T - 2, T - 1), (T - 1, T))
        aT_psum = [psS[2][:, 0:CH], psS[2][:, CH:GR], psS[2][:, CH:GR], psO[:, 0:P]]
        z_psum = [psS[0][:, 0:CH], psS[1][:, 0:CH], psO[:, P:P + D]]
        x2T_psum = [psS[2][:, 0:CH], psS[2][:, CH:GR]]
        cT_psum = [psO, psX]
        router_psum = psS[0][:, CH:CH + T * E]
        rank_psum, count_psum = psS[0][:, 0:T * E], psS[1][:, 0:E]

        POOL_LOW = (0, 2, 5)
        DVE_LOW = [n for n in range(NG) if n not in POOL_LOW]

        def ctx_rows(n):
            j0, j1 = n * 8, min(n * 8 + 8, QT)
            return stageN[:, j0 * D:j1 * D].rearrange("p (j d) -> p j d", d=D), j0, j1

        LOW_POOL = (3,)
        LOW_DVE = [e for e in range(NG) if e not in LOW_POOL]

        def wait_low(eng, t, e):
            if isinstance(t, int) and t == T - 1:
                eng.wait_ge(low_done, t * len(LOW_DVE) + e + 1)
            elif e in LOW_POOL:
                eng.wait_ge(low_pool_done, t * len(LOW_POOL) + LOW_POOL.index(e) + 1)
            else:
                eng.wait_ge(low_done, t * len(LOW_DVE) + LOW_DVE.index(e) + 1)

        def piece(e):
            n, w = len(tiles(e)), cols(e, GR)[1] - e * GR
            buf = Phl[:, e % 3, :, :] if e < NG - 1 else Ptail[:, :, :]
            return (buf.rearrange("p a w -> p (a w)"), buf[:, 0, 0:w], buf[:, 1, 0:w],
                    PT[:, 2 * e * TW:2 * e * TW + 2 * n, :])

        @block.sync
        def _(sp):
            sp.dma_start(x_sb[:, :, :], x.rearrange("(t p) d -> p t d", p=P)).then_inc(x_landed, 16)
            for n in range(NG):
                a, b = cols(n, GR)
                sp.dma_start(stageT[:, a:b], ctxT[:, a:b]).then_inc(qT_landed[n], 16)
            for n in range(NG):
                j0, j1 = n * 8, min(n * 8 + 8, QF)
                sp.dma_start(stageN[:, j0 * D:j1 * D].rearrange("p (j d) -> p j d", d=D),
                             ctx[j0 * P:j1 * P, :].rearrange("(j p) d -> p j d", p=P)).then_inc(qn_landed[n], 16)
            sp.wait_ge(tail_zeroed, 1)
            sp.dma_start(stageN[0:QTAIL, QF * D:QT * D], ctx[QF * P:Q, :]).then_inc(qtail_landed, 16)
            sp.dma_start(blr[:, :], b_l.rearrange("(o d) -> o d", o=1).broadcast_to([P, D])).then_inc(late_landed, 16)
            sp.dma_start(brs[:, :], br.rearrange("(o d) -> o d", o=1).broadcast_to([P, E])).then_inc(late_landed, 16)
            sp.dma_start(wrs[:, :], wr).then_inc(late_landed, 16)
            sp.dma_start(wl[:, :, :], wlT.rearrange("(k p) o -> p k o", p=P)).then_inc(late_landed, 16)
            sp.wait_ge(qTl_ready, len(DVE_LOW))
            sp.wait_ge(qTl_pool_ready, len(POOL_LOW))

            def load_w1(k):
                n = E // H
                sp.dma_start(stageT[:, k * WC:(k + 1) * WC].rearrange("p (e f) -> p e f", f=F),
                             w1[k * n:(k + 1) * n].rearrange("e h f -> h e f")).then_inc(w_landed[k], 16)

            def load_w2(k):
                n = E // H
                sp.wait_ge(w_low, k + 1)
                sp.dma_start(stageT[:, k * WC:(k + 1) * WC].rearrange("p (e k d) -> p e k d", k=FC, d=D),
                             w2[k * n:(k + 1) * n].rearrange("e (k p) d -> p e k d", p=P)).then_inc(w_landed[H + k], 16)

            sp.dma_start(x_re, x.rearrange("(t p) d -> p t d", p=P)).then_inc(x_re_landed, 16)
            for r in (0, 32):
                sp.dma_start(b12f[r:r + E, 0:F], b1).then_inc(b12_landed, 16)
                sp.dma_start(b12f[r:r + E, F:F + D], b2).then_inc(b12_landed, 16)
            load_w1(0)
            load_w1(1)

            def transpose(t, e, has_prev):
                wait_low(sp, t, e)
                if has_prev:
                    sp.wait_ge(pv_done, (t - 1) * NG + e + 1)
                else:
                    sp.wait_ge(qn_ready, e + 1)
                src, _, _, dst = piece(e)
                sp.dma_start_transpose(dst, src).then_inc(pT_landed[e], 16)

            for t in range(T):
                for e in range(NG):
                    transpose(t, e, t > 0)
                    if e == 2 and t < 2:
                        load_w1(t + 2)
                    elif e == 2 and t < 2 + H:
                        load_w2(t - 2)
                if 1 <= t <= NB // RING:
                    sp.wait_ge(empty_ready, 2)
                    sp.dma_start(xs[(t - 1) * RING * P:t * RING * P, :].rearrange("(k p) w -> p k w", p=P),
                                 empty[:, :].unsqueeze(1).broadcast_to([P, RING, ROW])).then_inc(slots_emptied, 16)
            sp.wait_ge(rows_sent, 16 * T)
            for i in range(RING):
                sp.dma_start(xblk[:, i, :], xs[i * P:(i + 1) * P, 0:D]).then_inc(x_blk_landed[i], 16)
            sp.dma_start(rest[:, :, :],
                         xs.rearrange("(b p) w -> p b w", p=P)[:, :, D:ROW]).then_inc(rest_landed, 16)
            with sp.Fori(0, NB // RING - 1) as k:
                for i in range(RING):
                    sp.wait_ge(xT_in_psum, k * RING + i + 1)
                    sp.dma_start(xblk[:, i, :],
                                 xs[bass.ds((k * RING + RING + i) * P, P), 0:D]).then_inc(x_blk_landed[i], 16)

        @block.gpsimd
        def _(pool):
            nc.gpsimd.memset(idf[:, :], 0.0).then_inc(consts_ready, 1)
            nc.gpsimd.memset(ones[:, :], 1.0).then_inc(consts_ready, 1)
            pool.wait_ge(consts_ready, 2)
            nc.gpsimd.affine_select(out=idf[:, :], in_=idf[:, :], compare_op=ALU.not_equal, fill=1.0, base=0,
                                    pattern=[[-1, P]], channel_multiplier=1).then_inc(consts_ready, 1)
            nc.gpsimd.memset(stageN[:, QF * D:QT * D], 0.0).then_inc(tail_zeroed, 1)
            nc.gpsimd.memset(Ptail[:, :, :], 0.0).then_inc(consts_ready, 1)
            for n in POOL_LOW:
                a, b = cols(n, GR)
                pool.wait_ge(qTh_ready, n + 1)
                nc.gpsimd.tensor_tensor(qTl[:, a:b], stageT[:, a:b], qTh[:, a:b],
                                        ALU.subtract).then_inc(qTl_pool_ready, 1)
            for n in range(NG):
                pool.wait_ge(qnh_ready, n + 1)
                src, j0, j1 = ctx_rows(n)
                nc.gpsimd.tensor_tensor(qn[:, j0:j1, 1, :], src, qn[:, j0:j1, 0, :],
                                        ALU.subtract).then_inc(qn_ready, 1)

            pool.wait_ge(late_gh_ready, 1)
            nc.gpsimd.tensor_tensor(gl[:, CH:N], g32[:, CH:N], gh[:, CH:N], ALU.subtract).then_inc(late_gl_ready, 1)

            step = [0]

            def then(ins):
                step[0] += 1
                ins.then_inc(route_consts, 1)
                pool.wait_ge(route_consts, step[0])

            def numbers(dst, n, pattern, base=0):
                then(nc.gpsimd.iota(ints[:, 0:n], pattern=pattern, base=base, channel_multiplier=0))
                then(nc.gpsimd.tensor_copy(dst, ints[:, 0:n]))

            numbers(iota_e[:, :], E, [[1, E]])
            numbers(kedge[:, :, :].rearrange("p e k -> p (e k)"), E * T, [[0, E], [P, T]])
            numbers(slot_no[:, :, :].rearrange("p b e -> p (b e)"), NB * E, [[P, NB], [0, E]])
            then(nc.gpsimd.memset(tri[:, :, :], float(P)))
            then(nc.gpsimd.affine_select(out=tri[:, :, :], in_=tri[:, :, :], compare_op=ALU.is_gt, fill=0.0, base=0,
                                         pattern=[[1, E], [-1, E]], channel_multiplier=0))
            then(nc.gpsimd.memset(ones16[:, :], 1.0))
            then(nc.gpsimd.affine_select(out=before[:, :], in_=ones16[:, :], compare_op=ALU.is_gt, fill=0.0, base=0,
                                         pattern=[[1, P]], channel_multiplier=-1))
            then(nc.gpsimd.iota(token[:, :], pattern=[[P, T]], base=0, channel_multiplier=1))

            def low_piece(t, e):
                pool.wait_ge(high_done, t * NG + e + 1)
                _, hi, lo, _ = piece(e)
                nc.gpsimd.tensor_tensor(lo, Pf[:, e % 3, 0:hi.shape[1]], hi, ALU.subtract).then_inc(low_pool_done, 1)

            for e in LOW_POOL:
                low_piece(0, e)
            pool.wait_ge(b12_landed, 64)
            then(nc.gpsimd.memset(b12[:, :], 0.0))
            then(nc.gpsimd.tensor_copy(b12[0:E, :], b12f[0:E, :]))
            then(nc.gpsimd.tensor_copy(b12t[32:32 + E, :], b12f[32:32 + E, :]))
            nc.gpsimd.tensor_tensor(b12[32:32 + E, :], b12f[32:32 + E, :], b12t[32:32 + E, :],
                                    ALU.subtract).then_inc(b12_ready, 1)
            pool.wait_ge(b12_ready, 1)
            nc.gpsimd.memset(empty[:, :], 0.0).then_inc(empty_ready, 1)
            pool.wait_ge(empty_ready, 1)
            nc.gpsimd.iota(empty[:, 2 * D:ROW].bitcast(I32), pattern=[[0, 1]], base=NOWHERE,
                           channel_multiplier=0).then_inc(empty_ready, 1)
            then(nc.gpsimd.memset(pick[:, :, :], 0.0))
            for r in (0, 32):
                then(nc.gpsimd.affine_select(out=pick[:, :, :], in_=pick[:, :, :], compare_op=ALU.not_equal, fill=1.0,
                                             base=-r, pattern=[[-1, E], [0, P]], channel_multiplier=1))

            def split(n):
                parts, at = (w1p, n * WC) if n < H else (w2p, (n - H) * WC)
                src = stageT[:, at:at + WC]
                pool.wait_ge(w_landed[n], 16)
                nc.gpsimd.tensor_copy(parts[:, 0, at:at + WC], src).then_inc(w_high, 1)
                pool.wait_ge(w_high, n + 1)
                nc.gpsimd.tensor_tensor(parts[:, 1, at:at + WC], src, parts[:, 0, at:at + WC],
                                        ALU.subtract).then_inc(w_low, 1)

            for e in LOW_POOL:
                low_piece(1, e)
            pool.wait_ge(x_re_landed, 16)
            pool.wait_ge(late_landed, 16 * NLATE)
            nc.gpsimd.tensor_tensor(x_re, x_re, blr[:, :].unsqueeze(1).broadcast_to([P, T, D]),
                                    ALU.add).then_inc(x_re_ready, 1)
            split(0)
            for t in range(2, T - 1):
                for e in LOW_POOL:
                    low_piece(t, e)
                split(t - 1)
            split(T - 2)
            split(T - 1)

            pool.wait_ge(x2n_ready, T)
            nc.gpsimd.tensor_copy(pay[:, :, 2 * D:ROW].bitcast(I32), token[:, :].unsqueeze(2)).then_inc(tokens_ready, 1)
            pool.wait_ge(tokens_ready, 1)
            pool.wait_ge(slots_emptied, 16 * (NB // RING))
            pool.wait_ge(pos_ready, 1)
            for t in range(T):
                pool.indirect_dma_start(out=xs, out_offset=bass.IndirectOffsetOnAxis(ap=pos[:, t:t + 1], axis=0),
                                        in_=pay[:, t, :], in_offset=None).then_inc(rows_sent, 16)
            for b in range(NB):
                i = b % RING
                pool.wait_ge(y_ready, b + 1)
                pool.indirect_dma_start(out=out, out_offset=bass.IndirectOffsetOnAxis(ap=ids[:, i:i + 1], axis=0),
                                        in_=yf[:, i, :], in_offset=None, bounds_check=N - 1,
                                        oob_is_err=False).then_inc(y_landed[i], 16)
            for i in range(RING):
                pool.wait_ge(y_landed[i], 16 * (NB // RING))

        @block.scalar
        def _(act):
            act.dma_start(vecs[:, 0:3], w3).then_inc(small_landed, 16)
            act.dma_start(b3s[:, :], b3.rearrange("(p o) -> p o", o=1)).then_inc(small_landed, 16)

            def deviation(n, t0, t1):
                act.wait_ge(var_ready, n)
                nc.scalar.activation(sc1[:, t0:t1], sc2[:, t0:t1], ACT.Sqrt).then_inc(sqrt_ready, 1)

            act.wait_ge(consts_ready, 2)
            nc.scalar.activation(warm[:, 0:1], ones[:, 0:1], ACT.Sqrt)
            deviation(1, 0, H)
            for n in range(NG):
                if n == 2:
                    deviation(2, H, T)
                a, b = cols(n, GR)
                act.wait_ge(qT_landed[n], 16)
                nc.scalar.copy(qTh[:, a:b], stageT[:, a:b]).then_inc(qTh_ready, 1)

            for n in range(NG):
                act.wait_ge(qn_landed[n], 16)
                if n == NG - 1:
                    act.wait_ge(qtail_landed, 16)
                src, j0, j1 = ctx_rows(n)
                nc.scalar.copy(qn[:, j0:j1, 0, :], src).then_inc(qnh_ready, 1)
            act.wait_ge(cT_in_psum, 2)
            act.wait_ge(g_ready, 2)
            for h in range(2):
                nc.scalar.copy(cT[:, h * CH:(h + 1) * CH], cT_psum[h][:, :]).then_inc(cT_ready, 1)
            act.wait_ge(vecs16_ready, 1)
            nc.scalar.activation(g32[:, CH:N], cT_psum[1][:, :], ACT.Identity, bias=vecs16[:, 1:2],
                                 scale=vecs16[:, 0:1]).then_inc(late_g_ready, 1)
            act.wait_ge(late_g_ready, 1)
            nc.scalar.copy(gh[:, CH:N], g32[:, CH:N]).then_inc(late_gh_ready, 1)

            def exp_piece(t, e):
                a, b = cols(e, GR)
                if e == 0:
                    act.wait_ge(negb_ready, t + 1)
                if e >= 3:
                    wait_low(act, t, e - 3)
                elif not isinstance(t, int) or t > 0:
                    wait_low(act, t - 1, (NG - 1, 4, 5)[e])
                nc.scalar.activation(Pf[:, e % 3, 0:b - a], S[:, a:b], ACT.Exp, bias=negb[:, bass.ds(t, 1)],
                                     accum_out=Lp[:, bass.ds(t * NG + e, 1)]).then_inc(exp_done, 1)

            def high(t, e, has_prev):
                act.wait_ge(exp_done, t * NG + e + 1)
                if e == NG - 1 and has_prev:
                    act.wait_ge(pT_landed[e], 16 * t)
                elif e == NG - 1:
                    act.wait_ge(consts_ready, 4)
                elif e >= 3:
                    act.wait_ge(pT_landed[e - 3], 16 * (t + 1))
                elif has_prev:
                    act.wait_ge(pT_landed[e + 3], 16 * t)
                _, hi, _, _ = piece(e)
                nc.scalar.copy(hi, Pf[:, e % 3, 0:hi.shape[1]]).then_inc(high_done, 1)

            def step(t, has_prev):
                for e in range(NG):
                    exp_piece(t, e)
                    high(t, e, has_prev)

            step(0, False)
            with act.Fori(1, T - 1) as t:
                step(t, True)
            for e in range(NG):
                exp_piece(T - 1, e)
                high(T - 1, e, True)
                if e == 2:
                    act.wait_ge(nM_ready, 1)
                    nc.scalar.activation(eb[:, :], Mrow[:, :], ACT.Exp, bias=nM[:, :],
                                         accum_out=es1[:, :]).then_inc(eb_ready, 1)
            act.wait_ge(eb_ready, 1)
            nc.scalar.activation(warm[:, 1:2], es1[:, :], ACT.Sqrt)
            deviation(3, 0, H)
            deviation(4, H, T)
            nc.scalar.activation(warm[:, 2:3], es1[:, :], ACT.Gelu)

            def x_high(b, i):
                act.wait_ge(xT_in_psum, b + 1)
                if not isinstance(b, int) or b >= RING:
                    act.wait_ge(h_in_psum, b - RING + 1)
                nc.scalar.copy(xTp[:, i, 0, :], psXT[i][:, 0:P]).then_inc(xT_high, 1)

            def hidden(b, i):
                act.wait_ge(h_in_psum, b + 1)
                if not isinstance(b, int) or b >= RING:
                    act.wait_ge(h_low, b - RING + 1)
                    act.wait_ge(y_in_psum, b - RING + 1)
                nc.scalar.activation(hf[:, i, :], psH[i], ACT.Gelu).then_inc(gelu_done, 1)
                act.wait_ge(gelu_done, b + 1)
                nc.scalar.copy(hp[:, i, 0, :], hf[:, i, :]).then_inc(h_high, 1)

            for i in range(RING):
                x_high(i, i)
            hidden(0, 0)
            hidden(1, 1)
            with act.Fori(0, NB // RING - 1) as k:
                for i in range(RING):
                    x_high(k * RING + RING + i, i)
                    hidden(k * RING + 2 + i, (2 + i) % RING)
            hidden(NB - 1, (NB - 1) % RING)

        @block.vector
        def _(dve):
            chain = [0]

            def link(ins):
                chain[0] += 1
                ins.then_inc(dve_chain, 1)
                dve.wait_ge(dve_chain, chain[0])

            norms = [0]

            def statistics(src, t0, t1):
                for t in range(t0, t1):
                    last = nc.vector.bn_stats(out=st[:, t, :], in_=src[:, t, :])
                link(last)
                for t in range(t0, t1):
                    last = nc.vector.bn_aggr(out=mv[:, t, :], in_=st[:, t, :])
                link(last)

            def normalise(src, dst, t0, t1, done):
                r = slice(t0, t1)
                nc.vector.tensor_scalar(sc2[:, r], mv[:, r, 1], EPS, None, ALU.add).then_inc(var_ready, 1)
                norms[0] += 1
                dve.wait_ge(sqrt_ready, norms[0])
                link(nc.vector.reciprocal(rstd[:, r], sc1[:, r]))
                link(nc.vector.tensor_tensor(sc1[:, r], rstd[:, r], rstd[:, r], ALU.mult))
                link(nc.vector.tensor_tensor(sc1[:, r], sc1[:, r], sc2[:, r], ALU.mult))
                link(nc.vector.tensor_scalar(sc1[:, r], sc1[:, r], -0.5, 1.5, ALU.mult, ALU.add))
                link(nc.vector.tensor_tensor(rstd[:, r], rstd[:, r], sc1[:, r], ALU.mult))
                for t in range(t0, t1):
                    nc.vector.tensor_scalar(dst[:, t, :], src[:, t, :], mv[:, t, 0:1], rstd[:, t:t + 1],
                                            ALU.subtract, ALU.mult).then_inc(done, 1)

            dve.wait_ge(x_landed, 16)
            statistics(x_sb, 0, H)
            normalise(x_sb, c_sb, 0, H, c_ready)
            dve.wait_ge(small_landed, 16 * NSMALL)
            nc.vector.tensor_scalar(vecs16[:, :], vecs[:, 0:2], GS, None, ALU.mult).then_inc(vecs16_ready, 1)
            dve.wait_ge(vecs16_ready, 1)
            nc.vector.tensor_copy(b3r[:, :], b3s[:, :].broadcast_to([3, T])).then_inc(g_ready, 1)

            dve.wait_ge(cT_in_psum, 1)
            link(nc.vector.tensor_scalar(g32[:, 0:CH], cT_psum[0][:, :], vecs16[:, 0:1], vecs16[:, 1:2],
                                         ALU.mult, ALU.add))
            link(nc.vector.tensor_copy(gh[:, 0:CH], g32[:, 0:CH]))
            nc.vector.tensor_tensor(gl[:, 0:CH], g32[:, 0:CH], gh[:, 0:CH], ALU.subtract).then_inc(g_ready, 1)

            statistics(x_sb, H, T)
            normalise(x_sb, c_sb, H, T, c_ready)

            def low_qT(n):
                a, b = cols(n, GR)
                dve.wait_ge(qTh_ready, n + 1)
                nc.vector.tensor_tensor(qTl[:, a:b], stageT[:, a:b], qTh[:, a:b],
                                        ALU.subtract).then_inc(qTl_ready, 1)

            def scores(u, n, has_prev):
                a, b = cols(n, GR)
                dve.wait_ge(scores_in_psum, u * NG + n + 1)
                if has_prev:
                    dve.wait_ge(exp_done, (u - 1) * NG + n + 1)
                    if n == 0:
                        dve.wait_ge(negb_ready, u)
                nc.vector.tensor_scalar(out=S[:, a:b], in0=psS[n % 3][:, 0:b - a], scalar1=1.0 / GS, scalar2=None,
                                        op0=ALU.mult, op1=ALU.max,
                                        accum_out=mxp[:, n:n + 1]).then_inc(scores_out, 1)

            def row_max(u):
                dve.wait_ge(scores_out, (u + 1) * NG)
                nc.vector.tensor_reduce(out=mx[:, bass.ds(u, 1)], in_=mxp[:, :], axis=AX.X,
                                        op=ALU.max).then_inc(max_parts, 1)
                dve.wait_ge(max_parts, u + 1)
                nc.vector.tensor_scalar(negb[:, bass.ds(u, 1)], mx[:, bass.ds(u, 1)], -1.0, LIFT,
                                        ALU.mult, ALU.add).then_inc(negb_ready, 1)

            def low(t, e):
                if e in LOW_POOL and not (isinstance(t, int) and t == T - 1):
                    return
                dve.wait_ge(high_done, t * NG + e + 1)
                _, hi, lo, _ = piece(e)
                nc.vector.tensor_tensor(lo, Pf[:, e % 3, 0:hi.shape[1]], hi, ALU.subtract).then_inc(low_done, 1)

            def attended(t, odd):
                nc.vector.tensor_reduce(out=Ls[:, :], in_=Lp[:, bass.ds(t * NG, NG)], axis=AX.X,
                                        op=ALU.add).then_inc(o_small, 1)
                dve.wait_ge(o_small, 3 * t + 1)
                nc.vector.reciprocal(Li[:, :], Ls[:, :]).then_inc(o_small, 1)
                dve.wait_ge(o_small, 3 * t + 2)
                dve.wait_ge(pv_done, (t + 1) * NG)
                nc.vector.tensor_scalar(otmp[:, :], psA[odd][:, 0:D], Li[:, :], None, ALU.mult).then_inc(o_small, 1)
                dve.wait_ge(o_small, 3 * t + 3)
                nc.vector.scalar_tensor_tensor(out=a_sb[:, bass.ts(t, D)], in0=psA[odd][:, D:2 * D], scalar=Li[:, :],
                                               in1=otmp[:, :], op0=ALU.mult, op1=ALU.add).then_inc(o_out, 1)

            def step(t, odd, has_prev, has_next):
                for e in range(NG):
                    if e == LAG and has_prev:
                        attended(t - 1, 1 - odd)
                    if has_next:
                        scores(t + 1, e, True)
                    low(t, e)
                if has_next:
                    row_max(t + 1)

            for n in range(NG):
                if n in DVE_LOW:
                    low_qT(n)
                if n >= 1:
                    scores(0, n - 1, False)
            scores(0, NG - 1, False)
            row_max(0)
            step(0, 0, False, True)
            dve.wait_ge(row_term_in_psum, 1)
            nc.vector.tensor_copy(row_term[:, :], psX[:, 0:T]).then_inc(row_term_ready, 1)
            with dve.Fori(1, T - 2, 2) as t:
                step(t, 1, True, True)
                step(t + 1, 0, True, True)

            def transposed(g):
                t0, t1 = TURNS[g]
                a, b = t0 * P, t1 * P
                dve.wait_ge(scores_in_psum, T * NG)
                dve.wait_ge(aT_in_psum, g + 1)
                link(nc.vector.tensor_copy(aT[:, a:b], aT_psum[g][:, 0:b - a]))
                nc.vector.tensor_tensor(caT[:, a:b], aT[:, a:b], cT[:, a:b], ALU.mult).then_inc(caT_ready, 1)

            def residual(g):
                dve.wait_ge(x_re_ready, 1)
                t0, t1 = GROUPS[g]
                dve.wait_ge(z_in_psum, g + 1)
                dve.wait_ge(scores_in_psum, T * NG)
                link(nc.vector.tensor_tensor(x1[:, t0:t1, :],
                                             z_psum[g][:, 0:(t1 - t0) * D].rearrange("p (t d) -> p t d", d=D),
                                             x_re[:, t0:t1, :], ALU.add))

            def router_operand(h):
                dve.wait_ge(x2T_in_psum, h + 1)
                nc.vector.tensor_copy(x2T[:, h * H * P:(h + 1) * H * P], x2T_psum[h][:, :]).then_inc(x2T_ready, 1)

            dve.wait_ge(max_parts, T)
            dve.wait_ge(row_term_ready, 1)
            link(nc.vector.tensor_tensor(Mrow[:, :], mx[:, :], row_term[:, :], ALU.add))
            nc.vector.tensor_reduce(out=m1[:, :], in_=Mrow[:, :], axis=AX.X, op=ALU.max).then_inc(m1_ready, 1)
            low(T - 1, 0)
            dve.wait_ge(m1T_in_psum, 1)
            nc.vector.tensor_reduce(out=m2[:, :], in_=psS[1][0:1, 0:P], axis=AX.X, op=ALU.max).then_inc(m2_ready, 1)
            transposed(0)
            low(T - 1, 1)
            dve.wait_ge(top_in_psum, 1)
            nc.vector.tensor_scalar(nM[:, :], psS[0][:, CH:CH + 1], -1.0, None, ALU.mult).then_inc(nM_ready, 1)
            transposed(1)
            low(T - 1, 2)
            low(T - 1, 3)
            attended(T - 2, 0)
            low(T - 1, 4)
            dve.wait_ge(q2c_in_psum, 1)
            link(nc.vector.reciprocal(Bi[:, :], psS[1][:, CH:CH + 1]))
            link(nc.vector.tensor_tensor(q2c[:, :], psS[0][:, CH:CH + 1], Bi[:, :], ALU.mult))
            dve.wait_ge(late_landed, 16 * NLATE)
            nc.vector.scalar_tensor_tensor(out=wc2[:, :], in0=wl[:, 3, :], scalar=q2c[:, :], in1=wl[:, 0, :],
                                           op0=ALU.mult, op1=ALU.add).then_inc(wc2_ready, 1)
            low(T - 1, 5)
            transposed(2)
            low(T - 1, 6)
            residual(0)
            statistics(x1, 0, H)
            normalise(x1, x2n, 0, H, x2n_ready)
            residual(1)
            statistics(x1, H, T - 1)
            attended(T - 1, 1)
            transposed(3)
            router_operand(0)
            residual(2)
            statistics(x1, T - 1, T)
            normalise(x1, x2n, H, T, x2n_ready)
            router_operand(1)
            dve.wait_ge(router_in_psum, 1)
            link(nc.vector.tensor_tensor(rsc[:, :, :], router_psum.rearrange("p (t e) -> p t e", e=E),
                                         brs[:, :].unsqueeze(1).broadcast_to([P, T, E]), ALU.add))
            link(nc.vector.tensor_reduce(out=rmx[:, :], in_=rsc[:, :, :], axis=AX.X, op=ALU.max))
            link(nc.vector.tensor_tensor(cand[:, :, :], rsc[:, :, :],
                                         rmx[:, :].unsqueeze(2).broadcast_to([P, T, E]), ALU.is_lt))
            dve.wait_ge(route_consts, ROUTE_CONSTS)
            iob = iota_e[:, :].unsqueeze(1).broadcast_to([P, T, E])
            link(nc.vector.scalar_tensor_tensor(out=cand[:, :, :], in0=cand[:, :, :], scalar=float(E), in1=iob,
                                                op0=ALU.mult, op1=ALU.add))
            link(nc.vector.tensor_reduce(out=rmx[:, :], in_=cand[:, :, :], axis=AX.X, op=ALU.min))
            nc.vector.tensor_tensor(oneh[:, :, :], iob, rmx[:, :].unsqueeze(2).broadcast_to([P, T, E]),
                                    ALU.is_equal).then_inc(chosen_ready, 1)
            dve.wait_ge(ranks_in_psum, 1)
            link(nc.vector.tensor_tensor(more[:, :, :], count_psum.unsqueeze(2).broadcast_to([P, E, T]),
                                         kedge[:, :, :], ALU.is_gt))
            link(nc.vector.tensor_reduce(out=nblk[:, :], in_=more[:, :, :], axis=AX.X, op=ALU.add))
            link(nc.vector.tensor_tensor(more[:, :, :], tri[:, :, :],
                                         nblk[:, :].unsqueeze(1).broadcast_to([P, E, E]), ALU.mult))
            link(nc.vector.tensor_reduce(out=sblk[:, :], in_=more[:, :, :], axis=AX.X, op=ALU.add))
            link(nc.vector.tensor_tensor(rank[:, :, :], rank_psum.rearrange("p (t e) -> p t e", e=E),
                                         sblk[:, :].unsqueeze(1).broadcast_to([P, T, E]), ALU.add))
            link(nc.vector.tensor_tensor(rank[:, :, :], rank[:, :, :], oneh[:, :, :], ALU.mult))
            link(nc.vector.tensor_reduce(out=posf[:, :], in_=rank[:, :, :], axis=AX.X, op=ALU.add))
            nc.vector.tensor_copy(pos[:, :], posf[:, :]).then_inc(pos_ready, 1)
            link(nc.vector.scalar_tensor_tensor(out=eblk[:, :], in0=nblk[:, :], scalar=float(P), in1=sblk[:, :],
                                                op0=ALU.mult, op1=ALU.add))
            link(nc.vector.tensor_tensor(past[:, :, :], eblk[:, :].unsqueeze(1).broadcast_to([P, NB, E]),
                                         slot_no[:, :, :], ALU.is_le))
            link(nc.vector.tensor_reduce(out=bexpf[:, :], in_=past[:, :, :], axis=AX.X, op=ALU.add))
            nc.vector.tensor_scalar(bexp[:, :], bexpf[:, :], float(E - 1), None, ALU.min).then_inc(experts_ready, 1)

            def x_low(b, i):
                dve.wait_ge(xT_high, b + 1)
                nc.vector.tensor_tensor(xTp[:, i, 1, :], psXT[i][:, 0:P], xTp[:, i, 0, :],
                                        ALU.subtract).then_inc(xT_low, 1)

            def hidden_low(b, i):
                dve.wait_ge(h_high, b + 1)
                nc.vector.tensor_tensor(hp[:, i, 1, :], hf[:, i, :], hp[:, i, 0, :], ALU.subtract).then_inc(h_low, 1)

            def finish(b, i):
                dve.wait_ge(y_in_psum, b + 1)
                nc.vector.tensor_tensor(yt[:, i, :], psY[i][:, 0:D], rest[:, bass.ds(b, 1), 0:D], ALU.add)\
                    .then_inc(y_part, 1)
                dve.wait_ge(y_part, b + 1)
                nc.vector.tensor_copy(ids[:, i:i + 1], rest[:, bass.ds(b, 1), D:D + 1].bitcast(I32))
                nc.vector.tensor_tensor(yf[:, i, :], psY[i][:, D:2 * D], yt[:, i, :], ALU.add).then_inc(y_ready, 1)

            for i in range(RING):
                x_low(i, i)
            hidden_low(0, 0)
            hidden_low(1, 1)
            dve.wait_ge(rest_landed, 16)
            for i in range(RING):
                x_low(RING + i, i)
                hidden_low(2 + i, (2 + i) % RING)
                finish(i, i)
            with dve.Fori(1, NB // RING - 1) as k:
                for i in range(RING):
                    x_low(k * RING + RING + i, i)
                    hidden_low(k * RING + 2 + i, (2 + i) % RING)
                    dve.wait_ge(y_landed[i], 16 * k)
                    finish(k * RING + i, i)
            hidden_low(NB - 1, (NB - 1) % RING)
            for b in range(NB - RING, NB):
                dve.wait_ge(y_landed[b % RING], 16 * (b // RING))
                finish(b, b % RING)

        @block.tensor
        def _(pe):
            pe.wait_ge(consts_ready, 3)

            def turn_c(h):
                for t in range(h * H, (h + 1) * H):
                    pe.wait_ge(c_ready, t + 1)
                    last = nc.tensor.transpose(cT_psum[h][:, (t - h * H) * P:(t - h * H + 1) * P], c_sb[:, t, :],
                                               idf[:, :])
                last.then_inc(cT_in_psum, 1)

            turn_c(0)

            def scores(u, c, has_prev):
                a, b = cols(c, CH)
                n = c // 2
                if c % 2 == 0:
                    if n >= 3:
                        pe.wait_ge(scores_out, u * NG + n - 2)
                    elif has_prev and n == 0:
                        pe.wait_ge(scores_out, u * NG)
                dst = psS[n % 3][:, (c % 2) * CH:(c % 2) * CH + b - a]
                g_h, g_l = gh[:, bass.ts(u, P)], gl[:, bass.ts(u, P)]
                nc.tensor.matmul(dst, g_h, qTh[:, a:b], start=True, stop=False)
                nc.tensor.matmul(dst, g_h, qTl[:, a:b], start=False, stop=False)
                last = nc.tensor.matmul(dst, g_l, qTh[:, a:b], start=False, stop=True)
                if c % 2 == 1 or c == NCH - 1:
                    last.then_inc(scores_in_psum, 1)

            def weighted(t, odd, e, has_prev):
                pe.wait_ge(pT_landed[e], 16 * (t + 1))
                if not has_prev:
                    pe.wait_ge(qn_ready, e + 1)
                if has_prev and e == 0 and (not isinstance(t, int) or t > 1):
                    pe.wait_ge(o_out, t - 1)
                n = len(tiles(e))
                for i, j in enumerate(tiles(e)):
                    nc.tensor.matmul(psA[odd][:, 0:2 * D], PT[:, 2 * e * TW + i, :],
                                     qn[:, j, :, :].rearrange("p a d -> p (a d)"),
                                     start=(j == 0), stop=False, skip_group_check=True)
                    last = nc.tensor.matmul(psA[odd][:, 0:D], PT[:, 2 * e * TW + n + i, :], qn[:, j, 0, :],
                                            start=False, stop=(j == QT - 1), skip_group_check=True)
                last.then_inc(pv_done, 1)

            def row_terms():
                pe.wait_ge(cT_ready, 2)
                pe.wait_ge(late_g_ready, 1)
                nc.tensor.matmul(psX[:, 0:T], ones[0:3, :], b3r[:, :], start=True, stop=False, skip_group_check=True)
                for t in range(T):
                    last = nc.tensor.matmul(psX[:, t:t + 1], cT[:, t * P:(t + 1) * P], vecs[:, 2:3],
                                            start=False, stop=(t == T - 1), skip_group_check=True)
                last.then_inc(row_term_in_psum, 1)

            def step(t, odd, has_prev, has_next):
                for e in range(NG):
                    if not has_prev and e == LAG:
                        row_terms()
                    if has_next:
                        for c in range(2 * e, min(2 * e + 2, NCH)):
                            scores(t + 1, c, True)
                    if e >= LAG:
                        weighted(t, odd, e - LAG, has_prev)
                    elif has_prev:
                        weighted(t - 1, 1 - odd, NG - LAG + e, True)

            pe.wait_ge(g_ready, 2)
            for c in range(NCH):
                if c % 2 == 0 and c // 2 in DVE_LOW:
                    pe.wait_ge(qTl_ready, DVE_LOW.index(c // 2) + 1)
                elif c % 2 == 0:
                    pe.wait_ge(qTl_pool_ready, POOL_LOW.index(c // 2) + 1)
                scores(0, c, False)
                if c == 3:
                    turn_c(1)
            step(0, 0, False, True)
            pe.wait_ge(qn_ready, NG)
            pe.wait_ge(row_term_ready, 1)
            pe.wait_ge(late_gl_ready, 1)
            with pe.Fori(1, T - 2, 2) as t:
                step(t, 1, True, True)
                step(t + 1, 0, True, True)

            def turn_a(g):
                t0, t1 = TURNS[g]
                pe.wait_ge(o_out, t1)
                if g == 2:
                    pe.wait_ge(caT_ready, 2)
                for t in range(t0, t1):
                    last = nc.tensor.transpose(aT_psum[g][:, (t - t0) * P:(t - t0 + 1) * P],
                                               a_sb[:, t * D:(t + 1) * D], idf[:, :])
                last.then_inc(aT_in_psum, 1)

            def linear_a(g):
                t0, t1 = TURNS[g]
                pe.wait_ge(caT_ready, g + 1)
                if g < 2:
                    pe.wait_ge(nM_ready, 1)
                pe.wait_ge(late_landed, 16 * NLATE)
                for t in range(t0, t1):
                    k = t // H if t < T - 1 else 2
                    dst = z_psum[k][:, (t - GROUPS[k][0]) * D:(t - GROUPS[k][0] + 1) * D]
                    r = slice(t * P, (t + 1) * P)
                    nc.tensor.matmul(dst, aT[:, r], wl[:, 1, :], start=(t == GROUPS[k][0]), stop=False,
                                     skip_group_check=True)
                    nc.tensor.matmul(dst, caT[:, r], wl[:, 2, :], start=False, stop=False, skip_group_check=True)

            def linear_c(g):
                t0, t1 = GROUPS[g]
                pe.wait_ge(wc2_ready, 1)
                for t in range(t0, t1):
                    last = nc.tensor.matmul(z_psum[g][:, (t - t0) * D:(t - t0 + 1) * D], cT[:, t * P:(t + 1) * P],
                                            wc2[:, :], start=False, stop=(t == t1 - 1), skip_group_check=True)
                last.then_inc(z_in_psum, 1)

            def turn_x2(h):
                pe.wait_ge(x2n_ready, (h + 1) * H)
                for t in range(h * H, (h + 1) * H):
                    last = nc.tensor.transpose(x2T_psum[h][:, (t - h * H) * P:(t - h * H + 1) * P], x2n[:, t, :],
                                               idf[:, :])
                last.then_inc(x2T_in_psum, 1)

            def router(h):
                pe.wait_ge(x2T_ready, h + 1)
                for t in range(h * H, (h + 1) * H):
                    last = nc.tensor.matmul(router_psum[:, t * E:(t + 1) * E], x2T[:, t * P:(t + 1) * P], wrs[:, :],
                                            start=True, stop=True)
                if h == 1:
                    last.then_inc(router_in_psum, 1)

            pe.wait_ge(scores_out, T * NG)
            turn_a(0)
            turn_a(1)
            pe.wait_ge(m1_ready, 1)
            nc.tensor.transpose(psS[1][0:1, 0:P], m1[:, :], idf[:, :]).then_inc(m1T_in_psum, 1)
            weighted(T - 2, 0, 3, True)
            pe.wait_ge(m2_ready, 1)
            nc.tensor.matmul(psS[0][:, CH:CH + 1], ones[0:1, :], m2[:, :], start=True, stop=True)\
                .then_inc(top_in_psum, 1)
            weighted(T - 2, 0, 4, True)
            linear_a(0)
            weighted(T - 2, 0, 5, True)
            linear_a(1)
            weighted(T - 2, 0, 6, True)
            pe.wait_ge(eb_ready, 1)
            for t in range(T):
                nc.tensor.matmul(psS[0][:, CH:CH + 1], c_sb[:, t, :], eb[:, t:t + 1], start=(t == 0), stop=(t == T - 1))
            nc.tensor.matmul(psS[1][:, CH:CH + 1], ones[:, :], es1[:, :], start=True, stop=True)\
                .then_inc(q2c_in_psum, 1)
            weighted(T - 1, 1, 0, True)
            weighted(T - 1, 1, 1, True)
            turn_a(2)
            linear_c(0)
            weighted(T - 1, 1, 2, True)
            weighted(T - 1, 1, 3, True)
            linear_a(2)
            linear_c(1)
            for e in (4, 5, 6):
                weighted(T - 1, 1, e, True)
            turn_x2(0)
            turn_a(3)
            linear_a(3)
            linear_c(2)
            router(0)
            turn_x2(1)
            router(1)

            pe.wait_ge(chosen_ready, 1)
            nc.tensor.matmul(rank_psum, before[:, :], oneh[:, :, :].rearrange("p t e -> p (t e)"),
                             start=True, stop=False, skip_group_check=True)
            for t in range(T - 1):
                nc.tensor.matmul(rank_psum[:, (t + 1) * E:T * E], ones16[:, :],
                                 oneh[:, t, :].unsqueeze(1).broadcast_to([P, T - 1 - t, E]),
                                 start=False, stop=(t == T - 2), skip_group_check=True)
            for t in range(T):
                last = nc.tensor.matmul(count_psum, ones16[:, :], oneh[:, t, :], start=(t == 0), stop=(t == T - 1))
            last.then_inc(ranks_in_psum, 1)

            def turn(lap, i):
                pe.wait_ge(x_blk_landed[i], 16 * (lap + 1))
                b = lap * RING + i
                ago = (1, 3, 2)[i]
                if not isinstance(b, int) or b >= ago:
                    pe.wait_ge(xT_low, b - ago + 1)
                nc.tensor.transpose(psXT[i][:, 0:P], xblk[:, i, :], idf[:, :]).then_inc(xT_in_psum, 1)

            expert_reg = [pe.alloc_register(f"expert{j}") for j in range(RING + 2)]

            def experts(b, n):
                pe.reg_load(expert_reg[0:n], bexp[0:1, bass.ds(b, n)])
                return [pe.snap(r, min_val=0, max_val=E - 1) for r in expert_reg[0:n]]

            def up(b, i, e, fresh):
                pe.wait_ge(xT_low, b + 1)
                if not fresh:
                    pe.wait_ge(gelu_done, b - RING + 1)
                pe.wait_ge(b12_ready, 1)
                for f in range(FC):
                    dst = psH[i][:, f * P:(f + 1) * P]
                    w_h, w_l = (w1p[:, a, bass.ds(e * F + f * P, P)] for a in range(2))
                    nc.tensor.matmul(dst, w_h, xTp[:, i, 0, :], start=True, stop=False)
                    nc.tensor.matmul(dst, w_h, xTp[:, i, 1, :], start=False, stop=False)
                    nc.tensor.matmul(dst, w_l, xTp[:, i, 0, :], start=False, stop=False)
                    last = nc.tensor.matmul(dst, b12[:, f * P:(f + 1) * P],
                                            pick[:, bass.ds(e, 1), :].rearrange("p o w -> p (o w)"),
                                            start=False, stop=True)
                last.then_inc(h_in_psum, 1)

            def down(b, i, e, fresh):
                pe.wait_ge(h_low, b + 1)
                if not fresh:
                    pe.wait_ge(y_ready, b - RING + 1)
                for f in range(FC):
                    nc.tensor.matmul(psY[i].rearrange("p (a d) -> p a d", a=2), hp[:, i, 0, f * P:(f + 1) * P],
                                     w2p[:, :, bass.ds(e * F + f * P, P)],
                                     start=(f == 0), stop=False, skip_group_check=True)
                    nc.tensor.matmul(psY[i][:, 0:D], hp[:, i, 1, f * P:(f + 1) * P],
                                     w2p[:, 0, bass.ds(e * F + f * P, P)],
                                     start=False, stop=False, skip_group_check=True)
                nc.tensor.matmul(psY[i][:, 0:D], pick[:, bass.ds(e, 1), :].rearrange("p o w -> p (o w)"),
                                 b12[:, F:F + D], start=False, stop=True, skip_group_check=True).then_inc(y_in_psum, 1)

            pe.wait_ge(b12_ready, 1)
            pe.wait_ge(route_consts, ROUTE_CONSTS)
            pe.wait_ge(w_low, T)
            for i in range(RING):
                turn(0, i)
            pe.wait_ge(experts_ready, 1)
            ex = experts(0, RING + 2)
            up(0, 0, ex[0], True)
            up(1, 1, ex[1], True)
            for i in range(RING):
                turn(1, i)
                up(2 + i, (2 + i) % RING, ex[2 + i], i == 0)
                down(i, i, ex[i], True)
            with pe.Fori(1, NB // RING - 1) as k:
                ex = experts(k * RING, RING + 2)
                for i in range(RING):
                    turn(k + 1, i)
                    up(k * RING + 2 + i, (2 + i) % RING, ex[2 + i], False)
                    down(k * RING + i, i, ex[i], False)
            ex = experts(NB - RING, RING)
            up(NB - 1, (NB - 1) % RING, ex[RING - 1], False)
            for b in range(NB - RING, NB):
                down(b, b % RING, ex[b - (NB - RING)], False)


def kernel(**inputs):
    import numpy as _np
    import concourse.bacc as _bacc
    from concourse import mybir as _mybir
    from concourse.bass_utils import run_bass_kernel_spmd as _run

    a = {k: _np.asarray(v) for k, v in inputs.items()}
    arrays = {
        "in_x": a["x"][0],
        "in_ctxT": a["ctx_1024"][0].T,
        "in_ctx": a["ctx_1024"][0],
        "in_w3": _np.stack([a["L0_xattn_w_cq"], a["L0_xattn_w_q"], a["L0_xattn_w_c"]], axis=1),
        "in_b3": _np.stack([a["L0_xattn_b_cq"], a["L0_xattn_b_c"], a["L0_xattn_b_q"]]),
        "in_wlT": a["L0_xattn_W_l"].T,
        "in_b_l": a["L0_xattn_b_l"],
        "in_wr": a["L0_ffn_wr"],
        "in_br": a["L0_ffn_br"],
        "in_w1": a["L0_ffn_w1"],
        "in_b1": a["L0_ffn_b1"],
        "in_w2": a["L0_ffn_w2"],
        "in_b2": a["L0_ffn_b2"],
    }
    arrays = {k: _np.ascontiguousarray(v) for k, v in arrays.items()}
    nc = _bacc.Bacc("TRN2", target_bir_lowering=False, num_devices=1)
    args = [nc.dram_tensor(k, v.shape, _mybir.dt.from_np(v.dtype), kind="ExternalInput").ap()
            for k, v in arrays.items()]
    args.append(nc.dram_tensor("out_x", arrays["in_x"].shape, _mybir.dt.float32, kind="ExternalOutput").ap())
    build(nc, *args)
    r = _run(nc, [arrays], core_ids=[0])
    return r.results[0]["out_x"][None]
```
